# Optimizing a Trainium2 kernel written in Bass

```python
import numpy as np
import jax
import jax.numpy as jnp

def _softmax(x, axis=-1):
    return jax.nn.softmax(x, axis=axis)

def _gelu(x):
    return jax.nn.gelu(x, approximate=True)

def _silu(x):
    return jax.nn.silu(x)

def _sigmoid(x):
    return jax.nn.sigmoid(x)

def _layernorm(x, axis=-1, eps=1e-05):
    m = jnp.mean(x, axis=axis, keepdims=True)
    v = jnp.var(x, axis=axis, keepdims=True)
    return (x - m) / jnp.sqrt(v + eps)

def _scatter_add(tgt, idx, src, axis=0):
    return tgt.at[idx].add(src)

def _segment_sum(src, seg, n):
    return jax.ops.segment_sum(src, seg, n)
kernel_name = 'mk_hybrid_d1_jaxref_r8_5693bb'

def setup_inputs(seed: int=0):
    np.random.seed(seed)
    _w = jnp.asarray

    def _L0_attn_a_setup():
        import jax, jax.numpy as jnp
        import numpy as np
        NUM_HEADS = 16
        FOCUS_FACTOR = 1.6
        HEAD_REGION = {0: 0, 1: 1, 2: 2}

        def _region_multipliers(seq_len: int, num_heads: int, factor: float) -> jnp.ndarray:
            first_end = max(1, seq_len // 3)
            second_end = max(first_end + 1, 2 * seq_len // 3)
            pos = jnp.arange(seq_len)
            regions = [pos < first_end, (pos >= first_end) & (pos < second_end), pos >= second_end]
            mult = np.ones((num_heads, seq_len), dtype=np.float32)
            mult = jnp.asarray(mult)
            for h, r in HEAD_REGION.items():
                if h < num_heads:
                    mult = mult.at[h].set(1.0 + (factor - 1.0) * regions[r].astype(jnp.float32))
            return mult
        key = jax.random.key(seed)
        k1, k2, k3, k4, k5 = jax.random.split(key, 5)
        B, S, D = (2, 256, 128)
        return {'hidden_states': jax.random.normal(k1, (B, S, D), dtype=jnp.float32), 'c_attn_w': jax.random.normal(k2, (D, 3 * D), dtype=jnp.float32) * 0.02, 'c_attn_b': jax.random.normal(k3, (3 * D,), dtype=jnp.float32) * 0.02, 'c_proj_w': jax.random.normal(k4, (D, D), dtype=jnp.float32) * 0.02, 'c_proj_b': jax.random.normal(k5, (D,), dtype=jnp.float32) * 0.02}
    _L0_attn_a_in = _L0_attn_a_setup()

    def _L0_attn_b_setup():
        import jax, jax.numpy as jnp
        import numpy as np
        HIDDEN = 128
        N_HEADS = 16
        D_HEAD = HIDDEN // N_HEADS

        def _rope(q, k):
            B, H, N, d = q.shape
            inv_freq = 1.0 / 10000.0 ** (jnp.arange(0, d, 2, dtype=jnp.float32) / d)
            pos = jnp.arange(N, dtype=jnp.float32)
            thetas = pos[:, None] * inv_freq[None, :]
            cos, sin = (jnp.cos(thetas), jnp.sin(thetas))

            def rot(x):
                xp = x.reshape(B, H, N, d // 2, 2)
                xx, xy = (xp[..., 0], xp[..., 1])
                rx = xx * cos - xy * sin
                ry = xx * sin + xy * cos
                return jnp.stack([rx, ry], axis=-1).reshape(B, H, N, d)
            return (rot(q), rot(k))
        key = jax.random.key(seed)
        ks = jax.random.split(key, 9)
        B, N, Hd = (4, 256, HIDDEN)
        s = 1.0 / np.sqrt(Hd)
        return {'x': jax.random.normal(ks[0], (B, N, Hd), jnp.float32), 'Wq': jax.random.normal(ks[1], (Hd, Hd), jnp.float32) * s, 'bq': jax.random.normal(ks[2], (Hd,), jnp.float32) * 0.02, 'Wk': jax.random.normal(ks[3], (Hd, Hd), jnp.float32) * s, 'bk': jax.random.normal(ks[4], (Hd,), jnp.float32) * 0.02, 'Wv': jax.random.normal(ks[5], (Hd, Hd), jnp.float32) * s, 'bv': jax.random.normal(ks[6], (Hd,), jnp.float32) * 0.02, 'Wo': jax.random.normal(ks[7], (Hd, Hd), jnp.float32) * s, 'bo': jax.random.normal(ks[8], (Hd,), jnp.float32) * 0.02}
    _L0_attn_b_in = _L0_attn_b_setup()

    def _L0_ffn_setup():
        import jax, jax.numpy as jnp
        import numpy as np
        D_IN, D_HID = (128, 512)

        def _ternary(key, shape):
            return jax.random.randint(key, shape, -1, 2).astype(jnp.float32)

        def _tlin(x, w, s):
            return jnp.einsum('bsi,oi->bso', x, w) * s
        key = jax.random.key(seed)
        ks = jax.random.split(key, 12)
        inv = lambda fan: 1.0 / np.sqrt(fan).astype(np.float32)
        return {'x': jax.random.normal(ks[0], (4, 256, D_IN), dtype=jnp.float32), 'w1_w': _ternary(ks[1], (D_HID, D_IN)), 'w1_s': jax.random.uniform(ks[2], (D_HID,), dtype=jnp.float32) * inv(D_IN), 'w2_w': _ternary(ks[3], (D_HID, D_IN)), 'w2_s': jax.random.uniform(ks[4], (D_HID,), dtype=jnp.float32) * inv(D_IN), 'h1_w': _ternary(ks[5], (D_HID, D_HID)), 'h1_s': jax.random.uniform(ks[6], (D_HID,), dtype=jnp.float32) * inv(D_HID), 'h2_w': _ternary(ks[7], (D_HID, D_HID)), 'h2_s': jax.random.uniform(ks[8], (D_HID,), dtype=jnp.float32) * inv(D_HID), 'w3_w': _ternary(ks[9], (D_IN, D_HID)), 'w3_s': jax.random.uniform(ks[10], (D_IN,), dtype=jnp.float32) * inv(D_HID)}
    _L0_ffn_in = _L0_ffn_setup()
    _d = {'L0_attn_a_hidden_states': _L0_attn_a_in['hidden_states'], 'L0_attn_a_c_attn_w': _L0_attn_a_in['c_attn_w'], 'L0_attn_a_c_attn_b': _L0_attn_a_in['c_attn_b'], 'L0_attn_a_c_proj_w': _L0_attn_a_in['c_proj_w'], 'L0_attn_a_c_proj_b': _L0_attn_a_in['c_proj_b'], 'L0_attn_b_Wq': _L0_attn_b_in['Wq'], 'L0_attn_b_bq': _L0_attn_b_in['bq'], 'L0_attn_b_Wk': _L0_attn_b_in['Wk'], 'L0_attn_b_bk': _L0_attn_b_in['bk'], 'L0_attn_b_Wv': _L0_attn_b_in['Wv'], 'L0_attn_b_bv': _L0_attn_b_in['bv'], 'L0_attn_b_Wo': _L0_attn_b_in['Wo'], 'L0_attn_b_bo': _L0_attn_b_in['bo'], 'L0_ffn_w1_w': _L0_ffn_in['w1_w'], 'L0_ffn_w1_s': _L0_ffn_in['w1_s'], 'L0_ffn_w2_w': _L0_ffn_in['w2_w'], 'L0_ffn_w2_s': _L0_ffn_in['w2_s'], 'L0_ffn_h1_w': _L0_ffn_in['h1_w'], 'L0_ffn_h1_s': _L0_ffn_in['h1_s'], 'L0_ffn_h2_w': _L0_ffn_in['h2_w'], 'L0_ffn_h2_s': _L0_ffn_in['h2_s'], 'L0_ffn_w3_w': _L0_ffn_in['w3_w'], 'L0_ffn_w3_s': _L0_ffn_in['w3_s']}
    _x0 = _d['L0_attn_a_hidden_states']
    _d['L0_attn_a_hidden_states'] = jax.random.normal(jax.random.fold_in(jax.random.key(seed), 1), (16, 512, 128), dtype=_x0.dtype)
    del _x0
    return _d

def reference(L0_attn_a_hidden_states, L0_attn_a_c_attn_w, L0_attn_a_c_attn_b, L0_attn_a_c_proj_w, L0_attn_a_c_proj_b, L0_attn_b_Wq, L0_attn_b_bq, L0_attn_b_Wk, L0_attn_b_bk, L0_attn_b_Wv, L0_attn_b_bv, L0_attn_b_Wo, L0_attn_b_bo, L0_ffn_w1_w, L0_ffn_w1_s, L0_ffn_w2_w, L0_ffn_w2_s, L0_ffn_h1_w, L0_ffn_h1_s, L0_ffn_h2_w, L0_ffn_h2_s, L0_ffn_w3_w, L0_ffn_w3_s):

    def _L0_attn_a_ref(hidden_states, c_attn_w, c_attn_b, c_proj_w, c_proj_b):
        import jax, jax.numpy as jnp
        import numpy as np
        NUM_HEADS = 16
        FOCUS_FACTOR = 1.6
        HEAD_REGION = {0: 0, 1: 1, 2: 2}

        def _region_multipliers(seq_len: int, num_heads: int, factor: float) -> jnp.ndarray:
            first_end = max(1, seq_len // 3)
            second_end = max(first_end + 1, 2 * seq_len // 3)
            pos = jnp.arange(seq_len)
            regions = [pos < first_end, (pos >= first_end) & (pos < second_end), pos >= second_end]
            mult = np.ones((num_heads, seq_len), dtype=np.float32)
            mult = jnp.asarray(mult)
            for h, r in HEAD_REGION.items():
                if h < num_heads:
                    mult = mult.at[h].set(1.0 + (factor - 1.0) * regions[r].astype(jnp.float32))
            return mult
        B, S, D = hidden_states.shape
        H = NUM_HEADS
        hd = D // H
        qkv = hidden_states @ c_attn_w + c_attn_b
        q, k, v = jnp.split(qkv, 3, axis=-1)

        def _reshape(x):
            return x.reshape(B, S, H, hd).transpose(0, 2, 1, 3)
        q, k, v = (_reshape(q), _reshape(k), _reshape(v))
        scores = jnp.einsum('bhqd,bhkd->bhqk', q, k) / jnp.sqrt(jnp.float32(hd))
        causal = jnp.tril(jnp.ones((S, S), dtype=bool))
        mask_value = jnp.finfo(scores.dtype).min
        scores = jnp.where(causal[None, None], scores, mask_value)
        attn = jax.nn.softmax(scores, axis=-1)
        mult = _region_multipliers(S, H, FOCUS_FACTOR)
        scaled = attn * mult[None, :, None, :]
        scaled = scaled / jnp.sum(scaled, axis=-1, keepdims=True)
        div_heads = jnp.zeros((H,), dtype=bool)
        for h in HEAD_REGION:
            if h < H:
                div_heads = div_heads.at[h].set(True)
        attn = jnp.where(div_heads[None, :, None, None], scaled, attn)
        out = jnp.einsum('bhqk,bhkd->bhqd', attn, v)
        out = out.transpose(0, 2, 1, 3).reshape(B, S, D)
        out = out @ c_proj_w + c_proj_b
        return out

    def _L0_attn_b_ref(x, Wq, bq, Wk, bk, Wv, bv, Wo, bo):
        import jax, jax.numpy as jnp
        import numpy as np
        HIDDEN = 128
        N_HEADS = 16
        D_HEAD = HIDDEN // N_HEADS

        def _rope(q, k):
            B, H, N, d = q.shape
            inv_freq = 1.0 / 10000.0 ** (jnp.arange(0, d, 2, dtype=jnp.float32) / d)
            pos = jnp.arange(N, dtype=jnp.float32)
            thetas = pos[:, None] * inv_freq[None, :]
            cos, sin = (jnp.cos(thetas), jnp.sin(thetas))

            def rot(x):
                xp = x.reshape(B, H, N, d // 2, 2)
                xx, xy = (xp[..., 0], xp[..., 1])
                rx = xx * cos - xy * sin
                ry = xx * sin + xy * cos
                return jnp.stack([rx, ry], axis=-1).reshape(B, H, N, d)
            return (rot(q), rot(k))
        B, N, _ = x.shape
        H, d = (N_HEADS, D_HEAD)
        q = (x @ Wq.T + bq).reshape(B, N, H, d).transpose(0, 2, 1, 3)
        k = (x @ Wk.T + bk).reshape(B, N, H, d).transpose(0, 2, 1, 3)
        v = (x @ Wv.T + bv).reshape(B, N, H, d).transpose(0, 2, 1, 3)
        q, k = _rope(q, k)
        scores = jnp.einsum('bhnd,bhmd->bhnm', q, k) / jnp.sqrt(jnp.asarray(d, x.dtype))
        attn = jax.nn.softmax(scores, axis=-1)
        out = jnp.einsum('bhnm,bhmd->bhnd', attn, v)
        out = out.transpose(0, 2, 1, 3).reshape(B, N, H * d)
        return out @ Wo.T + bo

    def _L0_ffn_ref(x, w1_w, w1_s, w2_w, w2_s, h1_w, h1_s, h2_w, h2_s, w3_w, w3_s):
        import jax, jax.numpy as jnp
        import numpy as np
        D_IN, D_HID = (128, 512)

        def _ternary(key, shape):
            return jax.random.randint(key, shape, -1, 2).astype(jnp.float32)

        def _tlin(x, w, s):
            return jnp.einsum('bsi,oi->bso', x, w) * s
        h = jax.nn.silu(_tlin(x, w1_w, w1_s)) * _tlin(x, w2_w, w2_s)
        h = jax.nn.gelu(_tlin(h, h1_w, h1_s), approximate=False)
        h = jax.nn.gelu(_tlin(h, h2_w, h2_s), approximate=False)
        return _tlin(h, w3_w, w3_s)
    x = L0_attn_a_hidden_states
    x = x + _L0_attn_a_ref(_layernorm(x, axis=-1), L0_attn_a_c_attn_w, L0_attn_a_c_attn_b, L0_attn_a_c_proj_w, L0_attn_a_c_proj_b)
    x = x + _L0_ffn_ref(_layernorm(x, axis=-1), L0_ffn_w1_w, L0_ffn_w1_s, L0_ffn_w2_w, L0_ffn_w2_s, L0_ffn_h1_w, L0_ffn_h1_s, L0_ffn_h2_w, L0_ffn_h2_s, L0_ffn_w3_w, L0_ffn_w3_s)
    x = x + _L0_attn_b_ref(_layernorm(x, axis=-1), L0_attn_b_Wq, L0_attn_b_bq, L0_attn_b_Wk, L0_attn_b_bk, L0_attn_b_Wv, L0_attn_b_bv, L0_attn_b_Wo, L0_attn_b_bo)
    x = x + _L0_ffn_ref(_layernorm(x, axis=-1), L0_ffn_w1_w, L0_ffn_w1_s, L0_ffn_w2_w, L0_ffn_w2_s, L0_ffn_h1_w, L0_ffn_h1_s, L0_ffn_h2_w, L0_ffn_h2_s, L0_ffn_w3_w, L0_ffn_w3_s)
    return x

_drawn_inputs = setup_inputs


def setup_inputs(seed=0):
    import zlib

    import numpy as np

    out = dict(_drawn_inputs(seed))
    spreads = {}
    factors = {}
    for name, (base, spread) in spreads.items():
        noise = np.random.default_rng([zlib.crc32(name.encode()), seed]).standard_normal(out[name].shape)
        drawn = base * np.exp(spread * noise) if base else spread * noise
        out[name] = jnp.asarray(drawn.astype(out[name].dtype))
    for name, factor in factors.items():
        out[name] = (out[name] * factor).astype(out[name].dtype)
    return out
```

```python
from contextlib import ExitStack

import concourse.bass as bass
import numpy as np
from concourse import mybir

F32 = mybir.dt.float32
BF16 = mybir.dt.bfloat16
ALU = mybir.AluOpType
ACT = mybir.ActivationFunctionType
AX = mybir.AxisListType

P = 128
B = 16
S = 512
D = 128
H = 16
HD = D // H
T = S // P
F = 512
FT = F // P
EPS = 1e-5
FOCUS = 1.6
FOCUS_HEADS = 3
SCALE = float(HD) ** -0.5

PAIRS = H // 2
HALF = PAIRS // 2
GROUPS = H // 4
TERMS = 6
KROWS = TERMS * HD
AUG = 2
UNITS = GROUPS * T
MAXES = PAIRS * T
MASKED = -1.0e30


def count(per, b, more=0):
    return per * b + more


def wait(eng, sem, value):
    if isinstance(value, int) and value <= 0:
        return
    eng.wait_ge(sem, value)


def wait_apart(eng, s, sem, value):
    if isinstance(value, int):
        wait(eng, sem, value)
        return
    eng.wait_ge(sem, value)
    eng.sem_inc(s["waited"], 1)


def program(nc, a, out):
    ctx = ExitStack()
    with ctx:
        def sb(name, shape, dt=F32):
            return ctx.enter_context(nc.sbuf_tensor(name, shape, dt))

        def sem(name):
            return ctx.enter_context(nc.semaphore(name))

        def dram(name, shape, dt):
            return nc.dram_tensor(name, shape, dt, kind="Internal").ap()

        m = {}
        m["x"] = sb("x", [P, B, T, D])
        m["ident"] = sb("ident", [P, P])
        m["ident_b"] = sb("ident_b", [P, P], BF16)
        m["mask_q"] = sb("mask_q", [P, P], BF16)
        m["mask_k"] = sb("mask_k", [P, P], BF16)
        m["half"] = sb("half", [P, T])
        m["stats"] = sb("stats", [P, T, 6])
        m["mv"] = sb("mv", [P, T, 2])
        m["var"] = sb("var", [P, T])
        m["rstd"] = sb("rstd", [P, T])
        m["xhat"] = sb("xhat", [P, T, D])
        m["xT"] = sb("xT", [P, S])
        m["weights"] = sb("weights", [P, 16, P])
        m["bias_col"] = sb("bias_col", [P, 4])
        m["bias_row"] = sb("bias_row", [P, 2, D])
        m["rope"] = sb("rope", [P, 4, S])
        m["stack_q"] = [sb(f"stack_q{c}", [P, PAIRS, S], BF16) for c in range(2)]
        m["stack_k"] = [sb(f"stack_k{c}", [P, PAIRS, S], BF16) for c in range(2)]
        m["v_aug"] = [sb(f"v_aug{c}", [P, T, H, 32]) for c in range(2)]
        m["v"] = sb("v", [P, T, D])
        m["qf"] = sb("qf", [P, 2, S])
        m["turned"] = sb("turned", [P, S])
        m["rest"] = sb("rest", [P, S])
        m["parts"] = sb("parts", [P, 2, 3, S], BF16)
        m["prob"] = [sb(f"prob{c}", [P, 4, S]) for c in range(2)]
        m["negmax"] = sb("negmax", [P, T, 2, PAIRS])
        m["nm_parts"] = sb("nm_parts", [P, T, 2, 2, 2, HALF], BF16)
        m["nm_rows"] = sb("nm_rows", [2 * 2 * HALF, 2, S], BF16)
        m["o_raw"] = sb("o_raw", [P, GROUPS, S])
        m["den"] = sb("den", [P, H * S // P])
        m["rden"] = sb("rden", [P, H * S // P])
        m["o_num"] = sb("o_num", [P, S])
        m["o_rden"] = sb("o_rden", [P, S])
        m["oT"] = sb("oT", [P, S])
        ps = [ctx.enter_context(nc.psum_tensor(f"ps{i}", [P, 512], F32)) for i in range(2)]
        m["ps_misc"], m["ps_out"] = ps
        m["ps_score"] = ctx.enter_context(nc.psum_tensor("ps_score", [P, 2, 512], F32))
        m["ps_max"] = ctx.enter_context(nc.psum_tensor("ps_max", [P, 4, 512], F32))
        m["ps_hid"], m["ps_a"], m["ps_b"] = m["ps_score"], m["ps_max"][:, 0:2], m["ps_max"][:, 2:4]
        m["focus"] = sb("focus", [P, T, FOCUS_HEADS])
        m["w_a"] = sb("w_a", [P, F])
        m["w_b"] = sb("w_b", [P, F])
        m["w_h1"] = sb("w_h1", [P, FT, F])
        m["w_h2"] = sb("w_h2", [P, FT, F])
        m["w_out"] = sb("w_out", [P, FT, D])
        m["s_col"] = sb("s_col", [P, 4, FT])
        m["s_half"] = sb("s_half", [P, FT])
        m["s_gate"] = sb("s_gate", [P, FT])
        m["s3_row"] = sb("s3_row", [P, D])
        m["tanh"] = sb("tanh", [P, 2, S])
        m["ut"] = sb("ut", [P, 2, S])
        m["h1"] = sb("h1", [P, FT, S])
        m["h2"], m["h3"] = m["prob"]
        m["y"] = sb("y", [P, T, D])
        m["d_stack"] = dram("d_stack", (2, 2, TERMS, HD, PAIRS, S), BF16)
        m["d_nm"] = dram("d_nm", (2, 2, 2, HALF, S), BF16)
        m["d_num"] = dram("d_num", (HD, 4, GROUPS, S), F32)
        m["d_den"] = dram("d_den", (4, GROUPS, S), F32)
        m["d_rden"] = dram("d_rden", (4, GROUPS, S), F32)

        setup(nc, ctx, sem, m, a)
        for stage in (lambda sem: attention(nc, sem, m, a, "a", causal=True),
                      lambda sem: ffn(nc, sem, m, a, "fa", None),
                      lambda sem: attention(nc, sem, m, a, "b", causal=False),
                      lambda sem: ffn(nc, sem, m, a, "fb", out)):
            own = []
            stage(lambda name: own.append(nc.alloc_semaphore(name=name)) or own[-1])
            nc.all_engine_barrier()
            nc.clear_and_free_semaphores(own)
            nc.all_engine_barrier()


def setup(nc, ctx, sem, m, a):
    ready = sem("setup_ready")
    loaded = sem("setup_loaded")
    m["waited"] = sem("waited")
    m["ffn_loaded"], m["ffn_loads"] = sem("ffn_loaded"), 7 * 16
    with nc.Block() as block:

        @block.gpsimd
        def _(pool):
            pool.memset(m["ident"][:], 0.0)
            pool.memset(m["ident_b"][:], 0.0)
            pool.memset(m["mask_q"][:], 0.0)
            pool.memset(m["mask_k"][:], 0.0).then_inc(ready, 1)
            pool.wait_ge(ready, 1)
            for name in ("ident", "ident_b"):
                pool.affine_select(out=m[name][:], in_=m[name][:], compare_op=ALU.not_equal, fill=1.0,
                                   base=0, pattern=[[-1, P]], channel_multiplier=1)
            pool.affine_select(out=m["mask_q"][:], in_=m["mask_q"][:], compare_op=ALU.is_ge, fill=MASKED,
                               base=0, pattern=[[1, P]], channel_multiplier=-1)
            pool.affine_select(out=m["mask_k"][:], in_=m["mask_k"][:], compare_op=ALU.is_ge, fill=MASKED,
                               base=0, pattern=[[-1, P]], channel_multiplier=1).then_inc(ready, 1)
            pool.wait_ge(ready, 2)

        @block.vector
        def _(dve):
            dve.memset(m["half"][:], -0.5)
            for c in range(2):
                for o in range(2):
                    dve.memset(m["stack_k"][c][64 * o + 32:64 * o + 64, :, :], 1.0)

        @block.sync
        def _(sp):
            for name in ("w_a", "w_b"):
                sp.dma_start(m[name][:], a[name]).then_inc(m["ffn_loaded"], 16)
            for name in ("w_h1", "w_h2", "w_out"):
                sp.dma_start(m[name][:], a[name].rearrange("(k p) f -> p k f", p=P)).then_inc(m["ffn_loaded"], 16)
            sp.dma_start(m["s_col"][:], a["s_col"]).then_inc(m["ffn_loaded"], 16)
            sp.dma_start(m["s3_row"][:], a["s3"].partition_broadcast(P)).then_inc(m["ffn_loaded"], 16)
            for lo, hi in ((0, 4), (4, 8), (8, 12), (12, 16)):
                sp.dma_start(m["x"][:, lo:hi], a["x"][lo:hi].rearrange("b (t p) d -> p b t d", p=P))\
                    .then_inc(loaded, 16)
            sp.wait_ge(loaded, 64)


def norm_stats(dve, m, s, b, first=None):
    wait(dve, s["xhat"], b)
    if first is not None:
        first()
    for t in range(T):
        last = dve.bn_stats(m["stats"][:, t], m["x"][:, b, t, :])
    last.then_inc(s["stats"], 1)
    wait_apart(dve, s, s["stats"], b + 1)
    for t in range(T):
        last = dve.bn_aggr(m["mv"][:, t], m["stats"][:, t])
    last.then_inc(s["mv"], 1)


def norm_rstd(pool, m, s, b):
    wait_apart(pool, s, s["mv"], b + 1)
    pool.tensor_scalar(m["var"][:], m["mv"][:, :, 1], EPS, None, ALU.add).then_inc(s["var"], 1)
    pool.wait_ge(s["var"], b + 1)
    wait(pool, s["xhat"], b)
    pool.tensor_tensor(m["rstd"][:], m["var"][:], m["half"][:], ALU.pow).then_inc(s["rstd"], 1)


def norm_apply(dve, m, s, b):
    dve.wait_ge(s["rstd"], b + 1)
    wait(dve, s["xT_ps"], b)
    for t in range(T):
        last = dve.tensor_scalar(m["xhat"][:, t, :], m["x"][:, b, t, :], m["mv"][:, t, 0:1],
                                 m["rstd"][:, t:t + 1], ALU.subtract, ALU.mult)
    last.then_inc(s["xhat"], 1)


def attention(nc, sem, m, a, tag, causal):
    w = a[tag]
    rotary = not causal
    names = ("loads", "focus", "ones", "stats", "mv", "var", "rstd", "xhat", "biased", "xT_ps", "xT", "q_ps", "q_main", "qr_ps",
             "q_turn", "q", "k_ps", "k_main", "kr_ps", "k_turn", "k", "v_ps", "v", "v_aug", "qh", "qr", "qm", "parts", "stored_q", "stored_k",
             "half0", "half1", "max_ps", "max", "nmh", "nm", "nm_ps0", "nm_ps1", "nm_row0", "nm_row1",
             "nm_out", "aug0", "aug1", "score", "prob", "pv", "o_raw", "o_out", "den", "rden", "rden_out",
             "o_in", "r_in", "oT", "proj", "resid")
    s = {n: sem(f"{tag}_{n}") for n in names}
    s["waited"] = m["waited"]
    W_Q, W_K, W_V, W_QR, W_KR, W_O = range(6)

    def width(j):
        return P * j if causal else 0

    def pipeline(eng, step):
        for n in range(4):
            step(n, n % 2)
        with eng.Fori(2, B // 2) as i:
            step(2 * i, 0)
            step(2 * i + 1, 1)
        for n in range(B, B + 3):
            step(n, n % 2)

    def on(n, lag):
        return not isinstance(n, int) or 0 <= n - lag < B

    misc = [("nm_row1", 2), ("xT", 0)]
    misc += [("q_main", 0), ("q_turn", 0), ("k_main", 0), ("k_turn", 0)] if rotary else [("q", 0), ("k", 0)]
    misc += [("v", 0), ("nm_row0", 1), ("resid", 3)]
    user = {name: i for i, (name, _) in enumerate(misc)}

    def misc_free(pe, n, name):
        index, back = user[name], 0
        while True:
            index -= 1
            if index < 0:
                index, back = index + len(misc), back + 1
                if isinstance(n, int) and n - back < 0:
                    return
            before, lag = misc[index]
            if on(n - back if isinstance(n, int) else n, lag):
                pe.wait_ge(s[before], n - back - lag + 1)
                return

    with nc.Block() as block:

        @block.sync
        def _(sp):
            sp.dma_start(m["weights"][:, 0:6, :], w["w"].rearrange("n k m -> k n m")).then_inc(s["loads"], 16)
            sp.dma_start(m["bias_col"][:], w["bias_col"]).then_inc(s["loads"], 16)
            for i, name in enumerate(("bias_v", "bias_o")):
                sp.dma_start(m["bias_row"][:, i, :], w[name].partition_broadcast(P)).then_inc(s["loads"], 16)
            if rotary:
                sp.dma_start(m["rope"][:], w["rope"].rearrange("n p t -> p n t")).then_inc(s["loads"], 16)

            else:
                sp.dma_start(m["focus"][:], a["focus"]).then_inc(s["focus"], 16)

            def aug(n, h, b, c):
                wait_apart(sp, s, s[f"nm_row{h}"], b + 1)
                sp.dma_start(m["d_nm"][h].rearrange("o c p t -> (o c p) t"), m["nm_rows"][:, h, :])\
                    .then_inc(s["nm_out"], 16)
                wait_apart(sp, s, s["nm_out"], count(32, b, 16 * (h + 1)))
                for o in range(2):
                    sp.dma_start(m["stack_q"][c][64 * o + KROWS:64 * o + KROWS + AUG, HALF * h:HALF * (h + 1), :],
                                 m["d_nm"][h, o]).then_inc(s[f"aug{h}"], 16)

            def step(n, c):
                if on(n, 2):
                    aug(n, 1, n - 2, c)
                if on(n, 3):
                    b = n - 3
                    wait_apart(sp, s, s["o_raw"], count(GROUPS, b, GROUPS))
                    for g in range(4):
                        sp.dma_start(m["d_num"][:, g], m["o_raw"][32 * g:32 * g + HD]).then_inc(s["o_out"], 16)
                        sp.dma_start(m["d_den"][g:g + 1], m["o_raw"][32 * g + HD:32 * g + HD + 1])\
                            .then_inc(s["o_out"], 16)
                    wait_apart(sp, s, s["o_out"], count(128, b, 128))
                    wait_apart(sp, s, s["rden"], b)
                    sp.dma_start(m["den"][:], m["d_den"].rearrange("g h (c t) -> (g h c) t", c=P // H))\
                        .then_inc(s["den"], 16)
                    wait_apart(sp, s, s["oT"], b)
                    sp.dma_start(m["o_num"][:], m["d_num"].rearrange("d g h t -> (d g h) t")).then_inc(s["o_in"], 16)
                    wait_apart(sp, s, s["rden"], b + 1)
                    sp.dma_start(m["d_rden"].rearrange("g h (c t) -> (g h c) t", c=P // H), m["rden"][:])\
                        .then_inc(s["rden_out"], 16)
                    wait_apart(sp, s, s["rden_out"], count(16, b, 16))
                    for d in range(HD):
                        sp.dma_start(m["o_rden"][H * d:H * (d + 1), :], m["d_rden"].rearrange("g h t -> (g h) t"))\
                            .then_inc(s["r_in"], 16)
                if on(n, 0):
                    b = n
                    for i, name in enumerate(("stored_q", "stored_k")):
                        wait_apart(sp, s, s["parts"], count(2, b, i + 1))
                        wait_apart(sp, s, s["half0"], count(64, b))
                        wait_apart(sp, s, s["half1"], count(64, b))
                        for o in range(2):
                            parts = m["parts"][64 * o:64 * (o + 1), i]
                            rows = m["d_stack"][i, o].rearrange("t d p n -> (d p) t n")
                            if i == 0:
                                for part, lo, hi in ((0, 0, 3), (1, 3, 5), (2, 5, 6)):
                                    sp.dma_start(rows[:, lo:hi],
                                                 parts[:, part:part + 1].broadcast_to([64, hi - lo, S]))\
                                        .then_inc(s[name], 16)
                            else:
                                for lo, hi in ((0, 3), (3, 5), (5, 6)):
                                    sp.dma_start(rows[:, lo:hi], parts[:, 0:hi - lo]).then_inc(s[name], 16)
                    wait_apart(sp, s, s["stored_q"], count(96, b, 96))
                    wait_apart(sp, s, s["stored_k"], count(96, b, 96))
                for h in range(2):
                    if on(n, 0):
                        b = n
                        wait_apart(sp, s, s["score"], count(4 * UNITS, b - 2, 2 * UNITS * (h + 1)))
                        for i, stack in enumerate((m["stack_q"][c], m["stack_k"][c])):
                            for o in range(2):
                                src = m["d_stack"][i, o].rearrange("t d p n -> (t d) p n")
                                sp.dma_start(stack[64 * o:64 * o + KROWS, HALF * h:HALF * (h + 1), :],
                                             src[:, HALF * h:HALF * (h + 1), :]).then_inc(s[f"half{h}"], 16)
                    if h == 0 and on(n, 1):
                        aug(n, 0, n - 1, 1 - c)

            pipeline(sp, step)

        @block.gpsimd
        def _(pool):
            for c in range(2):
                last = pool.memset(m["v_aug"][c][:], 1.0)
            last.then_inc(s["ones"], 1)
            pool.wait_ge(s["loads"], 80 if rotary else 64)

            def step(n, c):
                if on(n, 2):
                    negated_max_parts(n - 2, 1)
                if on(n, 0):
                    b = n
                    norm_rstd(pool, m, s, b)
                    pool.wait_ge(s["xhat"], b + 1)
                    bias = m["bias_row"][:, 1:2, :].broadcast_to([P, T, D])
                    pool.tensor_tensor(m["x"][:, b], m["x"][:, b], bias, ALU.add).then_inc(s["biased"], 1)
                    for i, name in enumerate(("q", "k")):
                        pool.wait_ge(s[name], b + 1)
                        wait_apart(pool, s, s["stored_q" if i == 0 else "stored_k"], count(96, b))
                        full, part = m["qf"][:, i], m["parts"][:, i]
                        pool.tensor_copy(part[:, 0], full).then_inc(s["qh"], 1)
                        pool.wait_ge(s["qh"], count(2, b, i + 1))
                        pool.tensor_tensor(m["rest"][:], full, part[:, 0], ALU.subtract).then_inc(s["qr"], 1)
                        wait_apart(pool, s, s["qr"], count(2, b, i + 1))
                        pool.tensor_copy(part[:, 1], m["rest"][:]).then_inc(s["qm"], 1)
                        pool.wait_ge(s["qm"], count(2, b, i + 1))
                        pool.tensor_tensor(part[:, 2], m["rest"][:], part[:, 1], ALU.subtract).then_inc(s["parts"], 1)
                if on(n, 1):
                    negated_max_parts(n - 1, 0)
                if on(n, 3):
                    b = n - 3
                    pool.wait_ge(s["o_in"], count(16, b, 16))
                    pool.wait_ge(s["r_in"], count(16 * HD, b, 16 * HD))
                    wait(pool, s["proj"], b)
                    pool.tensor_tensor(m["oT"][:], m["o_num"][:], m["o_rden"][:], ALU.mult).then_inc(s["oT"], 1)
                if on(n, 0):
                    b = n
                    pool.wait_ge(s["v"], b + 1)
                    wait_apart(pool, s, s["pv"], count(UNITS, b - 1))
                    to, v = m["v_aug"][c], m["v"][:].rearrange("p t (h d) -> p t h d", h=H)
                    lo = FOCUS_HEADS if causal else 0
                    if causal:
                        pool.tensor_tensor(to[:, :, 0:lo, 0:HD], v[:, :, 0:lo], to[:, :, 0:lo, HD:2 * HD], ALU.mult)
                    pool.tensor_copy(to[:, :, lo:H, 0:HD], v[:, :, lo:H]).then_inc(s["v_aug"], 1)

            def negated_max_parts(b, h):
                pool.wait_ge(s["max"], count(MAXES, b, MAXES // 2 * (h + 1)))
                wait_apart(pool, s, s[f"nm_ps{h}"], b)
                full = m["negmax"][:, :, :, HALF * h:HALF * (h + 1)]
                parts = m["nm_parts"][:, :, h]
                pool.tensor_copy(parts[:, :, :, 0], full).then_inc(s["nmh"], 1)
                pool.wait_ge(s["nmh"], count(2, b, h + 1))
                pool.tensor_tensor(parts[:, :, :, 1], full, parts[:, :, :, 0], ALU.subtract).then_inc(s["nm"], 1)

            if causal:
                pool.wait_ge(s["focus"], 16)
                pool.wait_ge(s["ones"], 1)
                for c in range(2):
                    last = pool.tensor_copy(m["v_aug"][c][:, :, 0:FOCUS_HEADS, :],
                                            m["focus"][:].rearrange("p t (h o) -> p t h o", o=1)
                                            .broadcast_to([P, T, FOCUS_HEADS, 32]))
                last.then_inc(s["ones"], 1)
                pool.wait_ge(s["ones"], 2)
            pipeline(pool, step)

        @block.vector
        def _(dve):
            dve.wait_ge(s["loads"], 80 if rotary else 64)

            def project(b, name, i):
                if not rotary:
                    dve.wait_ge(s[f"{name}_ps"], b + 1)
                    wait(dve, s["parts"], count(2, b, i - 1))
                    dve.tensor_scalar(m["qf"][:, i], m["ps_misc"][:], m["bias_col"][:, i:i + 1],
                                      1.0 if i else SCALE, ALU.add, ALU.mult).then_inc(s[name], 1)
                    return
                dve.wait_ge(s[f"{name}_ps"], b + 1)
                wait(dve, s["parts"], count(2, b, i - 1))
                dve.scalar_tensor_tensor(out=m["qf"][:, i], in0=m["ps_misc"][:], scalar=m["bias_col"][:, i:i + 1],
                                         in1=m["rope"][:, 2 * i], op0=ALU.add, op1=ALU.mult)\
                    .then_inc(s[f"{name}_main"], 1)

            def turn(b, name, i):
                dve.wait_ge(s[f"{name}r_ps"], b + 1)
                dve.scalar_tensor_tensor(out=m["turned"][:], in0=m["ps_misc"][:],
                                         scalar=m["bias_col"][:, 2 + i:3 + i], in1=m["rope"][:, 2 * i + 1],
                                         op0=ALU.add, op1=ALU.mult).then_inc(s[f"{name}_turn"], 1)
                dve.wait_ge(s[f"{name}_turn"], b + 1)
                dve.wait_ge(s[f"{name}_main"], b + 1)
                dve.tensor_tensor(m["qf"][:, i], m["qf"][:, i], m["turned"][:], ALU.add).then_inc(s[name], 1)

            def max_of(b, k):
                p, t = k // T, k % T
                if k % (MAXES // 2) == 0:
                    wait(dve, s["nm"], count(2, b - 1, 1 + k // (MAXES // 2)))
                dve.wait_ge(s["max_ps"], count(MAXES, b, k + 1))
                keys = P * (t + 1) if causal else S
                dve.tensor_reduce(m["negmax"][:, t, :, p], m["ps_max"][:, 2 * (k % 2):2 * (k % 2) + 2, 0:keys],
                                  AX.X, ALU.max, negate=True).then_inc(s["max"], 1)

            def step(n, c):
                for u in range(UNITS):
                    if on(n, 0):
                        if u == 0:
                            norm_stats(dve, m, s, n)
                        if u == 1:
                            norm_apply(dve, m, s, n)
                        if u == SLOT["q"] + 1:
                            project(n, "q", 0)
                        if u == SLOT["k"] + 1:
                            project(n, "k", 1)
                        if rotary and u == SLOT["qr"] + 1:
                            turn(n, "q", 0)
                        if rotary and u == SLOT["kr"] + 1:
                            turn(n, "k", 1)
                        if u == SLOT["v"] + 1:
                            dve.wait_ge(s["v_ps"], n + 1)
                            wait(dve, s["v_aug"], n)
                            dve.tensor_tensor(m["v"][:], m["ps_misc"][:].rearrange("p (t d) -> p t d", t=T),
                                              m["bias_row"][:, 0:1, :].broadcast_to([P, T, D]), ALU.add)\
                                .then_inc(s["v"], 1)
                    if on(n, 3):
                        b = n - 3
                        if u == 5:
                            dve.wait_ge(s["den"], count(16, b, 16))
                            wait(dve, s["rden_out"], count(16, b))
                            dve.reciprocal(m["rden"][:], m["den"][:]).then_inc(s["rden"], 1)
                        if u == SLOT["proj"] + 1:
                            dve.wait_ge(s["proj"], b + 1)
                            dve.wait_ge(s["biased"], b + 1)
                            dve.tensor_tensor(m["x"][:, b], m["ps_misc"][:].rearrange("p (t d) -> p t d", t=T),
                                              m["x"][:, b], ALU.add).then_inc(s["resid"], 1)
                    if on(n, 1):
                        max_of(n - 1, 2 * u)
                        max_of(n - 1, 2 * u + 1)

            pipeline(dve, step)

        @block.scalar
        def _(act):
            def nm_row(b, h):
                act.wait_ge(s[f"nm_ps{h}"], b + 1)
                wait(act, s["nm_out"], count(32, b - 1, 16 * (h + 1)))
                act.activation(m["nm_rows"][:, h, :], m["ps_misc"][0:16, 0:S // 2].bitcast(BF16), ACT.Copy)\
                    .then_inc(s[f"nm_row{h}"], 1)

            def group_out(b, G):
                act.wait_ge(s["pv"], count(UNITS, b, T * (G + 1)))
                wait(act, s["o_out"], count(128, b))
                act.activation(m["o_raw"][:, G], m["ps_out"][:], ACT.Copy).then_inc(s["o_raw"], 1)

            def step(n, c):
                for u in range(UNITS):
                    if u == SLOT["nm1"] + 1 and on(n, 2):
                        nm_row(n - 2, 1)
                    if u == SLOT["nm0"] + 1 and on(n, 1):
                        nm_row(n - 1, 0)
                    if u == SLOT["xT"] + 1 and on(n, 0):
                        act.wait_ge(s["xT_ps"], n + 1)
                        wait(act, s["v_ps"], n)
                        act.activation(m["xT"][:], m["ps_misc"][:], ACT.Copy).then_inc(s["xT"], 1)
                    for g in range(4):
                        if g == 2 and u == 1 and on(n, 3):
                            group_out(n - 3, GROUPS - 1)
                        if not on(n, 2):
                            continue
                        b = n - 2
                        if g == 2 and u % T == 1 and u > T:
                            group_out(b, u // T - 1)
                        if g == 0:
                            wait(act, s["pv"], count(UNITS, b, u - 1))
                        act.wait_ge(s["score"], count(4 * UNITS, b, 4 * u + g + 1))
                        lo = width(u % T)
                        act.activation(m["prob"][u % 2][:, g, lo:S], m["ps_score"][:, g % 2, 0:S - lo], ACT.Exp)\
                            .then_inc(s["prob"], 1)

            pipeline(act, step)

        @block.tensor
        def _(pe):
            pe.wait_ge(s["loads"], 80 if rotary else 64)

            def score(b, c, u, g):
                G, j = u // T, u % T
                p, o = 2 * G + g // 2, g % 2
                if g == 0 and u % (UNITS // 2) == 0:
                    h = u // (UNITS // 2)
                    pe.wait_ge(s[f"half{h}"], count(64, b, 64))
                    pe.wait_ge(s[f"aug{h}"], count(32, b, 32))
                wait(pe, s["prob"], count(4 * UNITS, b, 4 * u + g - 1))
                lo, rows = width(j), slice(64 * o, 64 * o + KROWS + AUG)
                last = pe.matmul(m["ps_score"][:, g % 2, 0:S - lo], m["stack_k"][c][rows, p, P * j:P * (j + 1)],
                                 m["stack_q"][c][rows, p, lo:S], start=True, stop=True)
                if causal:
                    last = pe.matmul(m["ps_score"][:, g % 2, 0:P], m["mask_k"][:], m["ident_b"][:],
                                     start=False, stop=True, skip_group_check=True)
                last.then_inc(s["score"], 1)

            def maxes(b, c, k):
                p, t = k // T, k % T
                if k % (MAXES // 2) == 0:
                    pe.wait_ge(s[f"half{k // (MAXES // 2)}"], count(64, b, 64))
                wait(pe, s["max"], count(MAXES, b, k - 1))
                keys = P * (t + 1) if causal else S
                for o in range(2):
                    rows = slice(64 * o, 64 * o + KROWS)
                    to = m["ps_max"][:, 2 * (k % 2) + o]
                    last = pe.matmul(to[:, 0:keys], m["stack_q"][c][rows, p, P * t:P * (t + 1)],
                                     m["stack_k"][c][rows, p, 0:keys], start=True, stop=True)
                if causal:
                    for o in range(2):
                        last = pe.matmul(m["ps_max"][:, 2 * (k % 2) + o, keys - P:keys], m["mask_q"][:],
                                         m["ident_b"][:], start=False, stop=True, skip_group_check=True)
                last.then_inc(s["max_ps"], 1)

            def weigh(b, c, u):
                G, j = u // T, u % T
                if u == 0:
                    pe.wait_ge(s["v_aug"], b + 1)
                if j == 0:
                    wait(pe, s["o_raw"], count(GROUPS, b, G))
                pe.wait_ge(s["prob"], count(4 * UNITS, b, 4 * u + 4))
                lo = width(j)
                for g in range(4):
                    last = pe.matmul(m["ps_out"][32 * g:32 * g + 32, lo:S], m["v_aug"][c][:, j, 4 * G + g, :],
                                     m["prob"][u % 2][:, g, lo:S], start=(j == 0), stop=(j == T - 1),
                                     skip_group_check=True)
                last.then_inc(s["pv"], 1)

            def turn_maxima(n, b, h):
                pe.wait_ge(s["nm"], count(2, b, h + 1))
                misc_free(pe, n, f"nm_row{h}")
                for t in range(T):
                    last = pe.transpose(m["ps_misc"][0:16, P // 2 * t:P // 2 * (t + 1)].bitcast(BF16),
                                        m["nm_parts"][:, t, h].rearrange("p a b c -> p (a b c)"), m["ident_b"][:])
                last.then_inc(s[f"nm_ps{h}"], 1)

            def linear(n, name, which, done):
                misc_free(pe, n, name)
                pe.wait_ge(s["xT"], n + 1)
                pe.matmul(m["ps_misc"][:], m["weights"][:, which], m["xT"][:], start=True, stop=True)\
                    .then_inc(s[done], 1)

            def misc_work(n, u):
                if u == SLOT["nm1"] and on(n, 2):
                    turn_maxima(n, n - 2, 1)
                if u == SLOT["nm0"] and on(n, 1):
                    turn_maxima(n, n - 1, 0)
                if u == SLOT["proj"] and on(n, 3):
                    pe.wait_ge(s["oT"], n - 3 + 1)
                    misc_free(pe, n, "resid")
                    for t in range(T):
                        last = pe.matmul(m["ps_misc"][:, P * t:P * (t + 1)], m["oT"][:, P * t:P * (t + 1)],
                                         m["weights"][:, W_O], start=True, stop=True)
                    last.then_inc(s["proj"], 1)
                if not on(n, 0):
                    return
                if u == SLOT["xT"]:
                    pe.wait_ge(s["xhat"], n + 1)
                    misc_free(pe, n, "xT")
                    for t in range(T):
                        last = pe.transpose(m["ps_misc"][:, P * t:P * (t + 1)], m["xhat"][:, t, :], m["ident"][:])
                    last.then_inc(s["xT_ps"], 1)
                if u == SLOT["q"]:
                    linear(n, "q_main" if rotary else "q", W_Q, "q_ps")
                if u == SLOT["k"]:
                    linear(n, "k_main" if rotary else "k", W_K, "k_ps")
                if rotary and u == SLOT["qr"]:
                    linear(n, "q_turn", W_QR, "qr_ps")
                if rotary and u == SLOT["kr"]:
                    linear(n, "k_turn", W_KR, "kr_ps")
                if u == SLOT["v"]:
                    misc_free(pe, n, "v")
                    for t in range(T):
                        last = pe.matmul(m["ps_misc"][:, P * t:P * (t + 1)], m["xT"][:, P * t:P * (t + 1)],
                                         m["weights"][:, W_V], start=True, stop=True)
                    last.then_inc(s["v_ps"], 1)

            def step(n, c):
                for u in range(UNITS):
                    if on(n, 2):
                        score(n - 2, c, u, 0)
                        score(n - 2, c, u, 1)
                    if on(n, 1):
                        maxes(n - 1, 1 - c, 2 * u)
                    if on(n, 2):
                        score(n - 2, c, u, 2)
                    if on(n, 1):
                        maxes(n - 1, 1 - c, 2 * u + 1)
                    if on(n, 2):
                        score(n - 2, c, u, 3)
                    if u == 0 and on(n, 3):
                        weigh(n - 3, 1 - c, UNITS - 1)
                    if u > 0 and on(n, 2):
                        weigh(n - 2, c, u - 1)
                    misc_work(n, u)

            pipeline(pe, step)


SLOT = {"nm1": 1, "xT": 2, "q": 3, "qr": 4, "k": 5, "kr": 6, "v": 7, "nm0": 9, "proj": 13}


def ffn(nc, sem, m, a, tag, out):
    names = ("halved", "stats", "mv", "var", "rstd", "xhat", "xT_ps", "xT", "a_ps", "b_ps", "tanh", "ut", "h1",
             "l2_ps", "h2", "l3_ps", "h3", "y_ps", "y", "resid", "stored")
    s = {n: sem(f"{tag}_{n}") for n in names}
    s["waited"] = m["waited"]

    def pipeline(eng, step):
        step(0)
        step(1)
        with eng.Fori(2, B) as n:
            step(n)
        step(B)

    def first(n):
        return not isinstance(n, int) or n < B

    def second(n):
        return not isinstance(n, int) or n > 0

    with nc.Block() as block:

        @block.sync
        def _(sp):
            def step(n):
                if second(n):
                    wait_apart(sp, s, s["resid"], n)
                    sp.dma_start(out[n - 1].rearrange("(t p) d -> p t d", p=P), m["x"][:, n - 1])\
                        .then_inc(s["stored"], 16)

            if out is not None:
                pipeline(sp, step)
                sp.wait_ge(s["stored"], 16 * B)

        @block.gpsimd
        def _(pool):
            pipeline(pool, lambda n: norm_rstd(pool, m, s, n) if first(n) else None)

        @block.vector
        def _(dve):
            dve.wait_ge(m["ffn_loaded"], m["ffn_loads"])
            dve.tensor_scalar(m["s_half"][:], m["s_col"][:, 0], 0.5, None, ALU.mult).then_inc(s["halved"], 1)
            dve.wait_ge(s["halved"], 1)
            dve.tensor_tensor(m["s_gate"][:], m["s_half"][:], m["s_col"][:, 1], ALU.mult).then_inc(s["halved"], 1)
            dve.wait_ge(s["halved"], 2)

            def step(n):
                if first(n):
                    norm_stats(dve, m, s, n)
                    norm_apply(dve, m, s, n)
                    for f in range(FT):
                        dve.wait_ge(s["tanh"], count(FT, n, f + 1))
                        dve.scalar_tensor_tensor(out=m["ut"][:, f % 2], in0=m["tanh"][:, f % 2], scalar=1.0,
                                                 in1=m["ps_a"][:, f % 2], op0=ALU.add, op1=ALU.mult)\
                            .then_inc(s["ut"], 1)
                        dve.wait_ge(s["ut"], count(FT, n, f + 1))
                        dve.wait_ge(s["b_ps"], count(FT, n, f + 1))
                        if f == 0:
                            wait(dve, s["l2_ps"], count(FT, n))
                        dve.scalar_tensor_tensor(out=m["h1"][:, f], in0=m["ps_b"][:, f % 2],
                                                 scalar=m["s_gate"][:, f:f + 1], in1=m["ut"][:, f % 2],
                                                 op0=ALU.mult, op1=ALU.mult).then_inc(s["h1"], 1)
                if second(n):
                    b = n - 1
                    wait(dve, s["resid"], b)
                    dve.wait_ge(s["y_ps"], b + 1)
                    dve.tensor_tensor(m["y"][:], m["ps_out"][:].rearrange("p (t d) -> p t d", t=T),
                                      m["s3_row"][:].rearrange("p (o d) -> p o d", o=1).broadcast_to([P, T, D]),
                                      ALU.mult).then_inc(s["y"], 1)
                    dve.wait_ge(s["y"], b + 1)
                    dve.tensor_tensor(m["x"][:, b], m["y"][:], m["x"][:, b], ALU.add).then_inc(s["resid"], 1)

            pipeline(dve, step)

        @block.scalar
        def _(act):
            act.wait_ge(s["halved"], 2)

            def gelu(b, ps, col, to, done, src, reader):
                for f in range(FT):
                    act.wait_ge(s[src], count(FT, b, f + 1))
                    if f == 0:
                        wait(act, s[reader], b if reader == "y_ps" else count(FT, b))
                    act.activation(m[to][:, f], m[ps][:, f % 2], ACT.Gelu, scale=m["s_col"][:, col, f:f + 1])\
                        .then_inc(s[done], 1)

            def step(n):
                if second(n):
                    gelu(n - 1, "ps_hid", 2, "h2", "h2", "l2_ps", "l3_ps")
                if first(n):
                    act.wait_ge(s["xT_ps"], n + 1)
                    wait(act, s["b_ps"], count(FT, n))
                    act.activation(m["xT"][:], m["ps_misc"][:], ACT.Copy).then_inc(s["xT"], 1)
                if second(n):
                    gelu(n - 1, "ps_hid", 3, "h3", "h3", "l3_ps", "y_ps")
                if first(n):
                    for f in range(FT):
                        act.wait_ge(s["a_ps"], count(FT, n, f + 1))
                        wait(act, s["ut"], count(FT, n, f - 1))
                        act.activation(m["tanh"][:, f % 2], m["ps_a"][:, f % 2], ACT.Tanh,
                                       scale=m["s_half"][:, f:f + 1]).then_inc(s["tanh"], 1)

            pipeline(act, step)

        @block.tensor
        def _(pe):
            pe.wait_ge(m["ffn_loaded"], m["ffn_loads"])

            def layer(b, w, src, ready, done, freed):
                for f in range(FT):
                    freed(f)
                    for k in range(FT):
                        if f == 0:
                            pe.wait_ge(s[ready], count(FT, b, k + 1))
                        last = pe.matmul(m["ps_hid"][:, f % 2], m[w][:, k, P * f:P * (f + 1)], m[src][:, k],
                                         start=(k == 0), stop=(k == FT - 1))
                    last.then_inc(s[done], 1)

            def step(n):
                if second(n):
                    b = n - 1
                    layer(b, "w_h1", "h1", "h1", "l2_ps",
                          lambda f: wait(pe, s["h3"], count(FT, b, f - 2)) if f < 2
                          else pe.wait_ge(s["h2"], count(FT, b, f - 1)))
                if first(n):
                    pe.wait_ge(s["xhat"], n + 1)
                    wait(pe, s["xT"], n)
                    for t in range(T):
                        last = pe.transpose(m["ps_misc"][:, P * t:P * (t + 1)], m["xhat"][:, t, :], m["ident"][:])
                    last.then_inc(s["xT_ps"], 1)
                if second(n):
                    layer(b, "w_h2", "h2", "h2", "l3_ps",
                          lambda f: pe.wait_ge(s["h2"], count(FT, b, f + 3)) if f < 2
                          else pe.wait_ge(s["h3"], count(FT, b, f - 1)))
                if first(n):
                    pe.wait_ge(s["xT"], n + 1)
                    for f in range(FT):
                        for name, done, reader in (("a", "a_ps", "ut"), ("b", "b_ps", "h1")):
                            wait(pe, s[reader], count(FT, n, f - 1))
                            pe.matmul(m[f"ps_{name}"][:, f % 2], m[f"w_{name}"][:, P * f:P * (f + 1)], m["xT"][:],
                                      start=True, stop=True).then_inc(s[done], 1)
                if second(n):
                    wait(pe, s["y"], b)
                    for t in range(T):
                        for k in range(FT):
                            if t == 0:
                                pe.wait_ge(s["h3"], count(FT, b, k + 1))
                            last = pe.matmul(m["ps_out"][:, P * t:P * (t + 1)], m["h3"][:, k, P * t:P * (t + 1)],
                                             m["w_out"][:, k], start=(k == 0), stop=(k == FT - 1))
                    last.then_inc(s["y_ps"], 1)

            pipeline(pe, step)


def rows_of_heads():
    return np.array([(2 * p + o) * HD + d for o in range(2) for d in range(HD) for p in range(PAIRS)])


def rows_of_output():
    return np.array([(4 * G + g) * HD + d for d in range(HD) for g in range(4) for G in range(GROUPS)])


def rope_tables():
    inv = np.float32(1.0) / np.float32(10000.0) ** (np.arange(0, HD, 2, dtype=np.float32) / np.float32(HD))
    theta = np.arange(S, dtype=np.float32)[:, None] * inv[None, :].astype(np.float32)
    d = rows_of_heads() % HD
    cos, sin = np.cos(theta).T[d // 2], np.sin(theta).T[d // 2]
    sin = np.where((d % 2 == 0)[:, None], -sin, sin)
    scale = np.float32(SCALE)
    return np.stack([cos * scale, sin * scale, cos, sin]).astype(np.float32)


def focus_weights():
    edges = [0, max(1, S // 3), max(max(1, S // 3) + 1, 2 * S // 3), S]
    w = np.ones((P, T, FOCUS_HEADS), np.float32)
    for r in range(FOCUS_HEADS):
        for tok in range(edges[r], edges[r + 1]):
            w[tok % P, tok // P, r] = FOCUS
    return w


def turned_feature(f):
    return f ^ 1


def layout(i):
    q, o = rows_of_heads(), rows_of_output()
    qr = turned_feature(q)
    r = {"x": i["L0_attn_a_hidden_states"], "focus": focus_weights(), "rope": rope_tables()}
    w, bias = i["L0_attn_a_c_attn_w"], i["L0_attn_a_c_attn_b"]
    wq, wk, wv = w[:, 0:D], w[:, D:2 * D], w[:, 2 * D:3 * D]
    bq, bk = bias[0:D], bias[D:2 * D]
    r["a_w"] = np.stack([wq[:, q], wk[:, q], wv, wq[:, qr], wk[:, qr], i["L0_attn_a_c_proj_w"][o]])
    r["a_bias_col"] = np.stack([bq[q], bk[q], bq[qr], bk[qr]], 1)
    r["a_bias_v"], r["a_bias_o"] = bias[2 * D:3 * D], i["L0_attn_a_c_proj_b"]
    wq, wk, wv, wo = (i[f"L0_attn_b_W{n}"].T for n in "qkvo")
    bq, bk = i["L0_attn_b_bq"], i["L0_attn_b_bk"]
    r["b_w"] = np.stack([wq[:, q], wk[:, q], wv, wq[:, qr], wk[:, qr], wo[o]])
    r["b_bias_col"] = np.stack([bq[q], bk[q], bq[qr], bk[qr]], 1)
    r["b_bias_v"], r["b_bias_o"] = i["L0_attn_b_bv"], i["L0_attn_b_bo"]
    r["w_a"], r["w_b"] = i["L0_ffn_w1_w"].T, i["L0_ffn_w2_w"].T
    r["w_h1"], r["w_h2"], r["w_out"] = i["L0_ffn_h1_w"].T, i["L0_ffn_h2_w"].T, i["L0_ffn_w3_w"].T
    r["s_col"] = np.stack([i[f"L0_ffn_{n}_s"].reshape(FT, P).T for n in ("w1", "w2", "h1", "h2")], 1)
    r["s3"] = i["L0_ffn_w3_s"]
    return {k: np.ascontiguousarray(v) for k, v in r.items()}


def kernel(**inputs):
    import concourse.bacc as bacc
    from concourse.bass_utils import run_bass_kernel_spmd

    arrays = {f"in_{k}": v for k, v in layout({k: np.asarray(v) for k, v in inputs.items()}).items()}
    nc = bacc.Bacc("TRN2", target_bir_lowering=False, num_devices=1)
    a = {k[3:]: nc.dram_tensor(k, v.shape, mybir.dt.from_np(v.dtype), kind="ExternalInput").ap()
         for k, v in arrays.items()}
    for tag in "ab":
        a[tag] = {n: a[f"{tag}_{n}"] for n in ("w", "bias_col", "bias_v", "bias_o")}
        a[tag]["rope"] = a["rope"]
    out = nc.dram_tensor("out", (B, S, D), F32, kind="ExternalOutput").ap()
    program(nc, a, out)
    r = run_bass_kernel_spmd(nc, [arrays], core_ids=[0])
    return r.results[0]["out"]
```

```python
from contextlib import ExitStack

import concourse.bass as bass
import numpy as np
from concourse import mybir

F32 = mybir.dt.float32
F32R = mybir.dt.float32r
I32 = mybir.dt.int32
BF16 = mybir.dt.bfloat16
ALU = mybir.AluOpType
ACT = mybir.ActivationFunctionType
AX = mybir.AxisListType

P = 128
B = 16
S = 512
D = 128
H = 16
HD = D // H
T = S // P
F = 512
FT = F // P
EPS = 1e-5
FOCUS = 1.6
FOCUS_HEADS = 3
SCALE = float(HD) ** -0.5

PAIRS = H // 2
HALF = PAIRS // 2
GROUPS = H // 4
TERMS = 6
KROWS = TERMS * HD
AUG_AT = 2 * KROWS
AUG = 2
UNITS = GROUPS * T
MAXES = PAIRS * T
MASKED = -1.0e30

W_AT = {"a": 0, "b": F, "h1": 2 * F, "h2": 2 * F + FT * F, "out": 2 * F + 2 * FT * F}
W_COLS = W_AT["out"] + FT * D
W_PIECES = [("prob0", "h1", FT * F), ("prob1", "h2", FT * F), ("o_raw", "a", F), ("o_raw", "b", F), ("o_raw", "out", FT * D)]


def count(per, b, more=0):
    return per * b + more


def wait(eng, sem, value):
    if isinstance(value, int) and value <= 0:
        return
    eng.wait_ge(sem, value)


def wait_apart(eng, s, sem, value):
    if isinstance(value, int):
        wait(eng, sem, value)
        return
    eng.wait_ge(sem, value)
    eng.sem_inc(s["waited"], 1)


def program(nc, a, out):
    ctx = ExitStack()
    with ctx:
        def sb(name, shape, dt=F32):
            return ctx.enter_context(nc.sbuf_tensor(name, shape, dt))

        def sem(name):
            return ctx.enter_context(nc.semaphore(name))

        def dram(name, shape, dt):
            return nc.dram_tensor(name, shape, dt, kind="Internal").ap()

        m = {}
        m["x"] = sb("x", [P, B, T, D])
        m["ident"] = sb("ident", [P, P])
        m["ident_b"] = sb("ident_b", [P, P], BF16)
        m["mask_q"] = sb("mask_q", [P, P], BF16)
        m["mask_k"] = sb("mask_k", [P, P], BF16)
        m["half"] = sb("half", [P, T])
        m["stats"] = sb("stats", [P, T, 6])
        m["mv"] = sb("mv", [P, T, 2])
        m["var"] = sb("var", [P, T])
        m["rstd"] = sb("rstd", [P, T])
        m["xhat"] = sb("xhat", [P, T, D])
        ps = [ctx.enter_context(nc.psum_tensor(f"ps{i}", [P, 512], F32)) for i in range(2)]
        m["ps_misc"], m["ps_out"] = ps
        m["ps_score"] = ctx.enter_context(nc.psum_tensor("ps_score", [P, 2, 512], F32))
        m["ps_max"] = ctx.enter_context(nc.psum_tensor("ps_max", [P, 4, 512], F32))
        m["stack_k"] = [sb(f"stack_k{c}", [P, 2, PAIRS, S], BF16) for c in range(2)]
        m["aug_ones"] = sb("aug_ones", [P, 2, S], BF16)
        m["ps_hid"], m["ps_a"], m["ps_b"] = m["ps_score"], m["ps_max"][:, 0:2], m["ps_max"][:, 2:4]
        m["focus"] = sb("focus", [P, T, FOCUS_HEADS])
        m["w_hi"] = sb("w_hi", [P, W_COLS], F32R)
        m["w_lo"] = sb("w_lo", [P, W_COLS], F32R)
        m["w_rest"] = sb("w_rest", [P, len(W_PIECES)])
        m["s_col"] = sb("s_col", [P, 4, FT])
        m["s3_row"] = sb("s3_row", [P, D])
        m["d_stack"] = dram("d_stack", (2, 2, TERMS, HD, PAIRS, S), BF16)
        m["d_nm"] = dram("d_nm", (2, 2, 2, HALF, S), BF16)
        m["d_num"] = dram("d_num", (HD, 4, GROUPS, S), F32)
        m["d_den"] = dram("d_den", (4, GROUPS, S), F32)
        m["d_rden"] = dram("d_rden", (4, GROUPS, S), F32)

        setup(nc, ctx, sem, m, a)
        for stage in (lambda sem: attention(nc, sem, m, a, "a", causal=True),
                      lambda sem: ffn(nc, sem, m, a, "fa", None),
                      lambda sem: attention(nc, sem, m, a, "b", causal=False),
                      lambda sem: ffn(nc, sem, m, a, "fb", out)):
            own = []
            stage(lambda name: own.append(nc.alloc_semaphore(name=name)) or own[-1])
            nc.all_engine_barrier()
            nc.clear_and_free_semaphores(own)
            nc.all_engine_barrier()


def setup(nc, ctx, sem, m, a):
    ready = sem("setup_ready")
    loaded = sem("setup_loaded")
    zeroed = sem("setup_zeroed")
    m["waited"] = sem("waited")
    m["ffn_loaded"], m["ffn_loads"] = sem("ffn_loaded"), 2 * 16
    with nc.Block() as block:

        @block.gpsimd
        def _(pool):
            pool.memset(m["ident"][:], 0.0)
            pool.memset(m["aug_ones"][:], 0.0)
            pool.memset(m["ident_b"][:], 0.0)
            pool.memset(m["mask_q"][:], 0.0)
            pool.memset(m["mask_k"][:], 0.0).then_inc(ready, 1)
            pool.wait_ge(ready, 1)
            for name in ("ident", "ident_b"):
                last = pool.affine_select(out=m[name][:], in_=m[name][:], compare_op=ALU.not_equal, fill=1.0,
                                          base=0, pattern=[[-1, P]], channel_multiplier=1)
            last.then_inc(ready, 1)
            for o, (base, step) in enumerate(((-AUG, 1), (AUG - 1, -1))):
                rows = m["aug_ones"][AUG_AT:AUG_AT + 2 * AUG, o]
                pool.wait_ge(ready, 2 + o)
                pool.affine_select(out=rows, in_=rows, compare_op=ALU.is_ge, fill=1.0, base=base,
                                   pattern=[[0, S]], channel_multiplier=step).then_inc(ready, 1)
            pool.wait_ge(ready, 4)
            pool.affine_select(out=m["mask_q"][:], in_=m["mask_q"][:], compare_op=ALU.is_ge, fill=MASKED,
                               base=0, pattern=[[1, P]], channel_multiplier=-1)
            pool.affine_select(out=m["mask_k"][:], in_=m["mask_k"][:], compare_op=ALU.is_ge, fill=MASKED,
                               base=0, pattern=[[-1, P]], channel_multiplier=1).then_inc(ready, 1)
            pool.wait_ge(ready, 5)

        @block.vector
        def _(dve):
            dve.memset(m["half"][:], -0.5)
            dve.memset(m["ps_out"][:], 0.0)
            for c in range(2):
                last = dve.memset(m["stack_k"][c][:], 0.0)
            last.then_inc(zeroed, 1)
            dve.wait_ge(zeroed, 1)
            dve.wait_ge(ready, 4)
            for c in range(2):
                for o in range(2):
                    rows = slice(AUG_AT, AUG_AT + 2 * AUG)
                    dve.tensor_copy(m["stack_k"][c][rows, o],
                                    m["aug_ones"][rows, o:o + 1].broadcast_to([2 * AUG, PAIRS, S]))

        @block.sync
        def _(sp):
            sp.dma_start(m["s_col"][:], a["s_col"]).then_inc(m["ffn_loaded"], 16)
            sp.dma_start(m["s3_row"][:], a["s3"].partition_broadcast(P)).then_inc(m["ffn_loaded"], 16)
            for lo, hi in ((0, 4), (4, 8), (8, 12), (12, 16)):
                sp.dma_start(m["x"][:, lo:hi], a["x"][lo:hi].rearrange("b (t p) d -> p b t d", p=P))\
                    .then_inc(loaded, 16)
            sp.wait_ge(loaded, 64)


def norm_stats(dve, m, s, b, first=None):
    wait(dve, s["xhat"], b)
    if first is not None:
        first()
    for t in range(T):
        last = dve.bn_stats(m["stats"][:, t], m["x"][:, b, t, :])
    last.then_inc(s["stats"], 1)
    wait_apart(dve, s, s["stats"], b + 1)
    for t in range(T):
        last = dve.bn_aggr(m["mv"][:, t], m["stats"][:, t])
    last.then_inc(s["mv"], 1)


def norm_rstd(pool, m, s, b):
    wait_apart(pool, s, s["mv"], b + 1)
    pool.tensor_scalar(m["var"][:], m["mv"][:, :, 1], EPS, None, ALU.add).then_inc(s["var"], 1)
    pool.wait_ge(s["var"], b + 1)
    wait(pool, s["xhat"], b)
    pool.tensor_tensor(m["rstd"][:], m["var"][:], m["half"][:], ALU.pow).then_inc(s["rstd"], 1)


def norm_apply(dve, m, s, b):
    dve.wait_ge(s["rstd"], b + 1)
    wait(dve, s["xT_ps"], b)
    for t in range(T):
        last = dve.tensor_scalar(m["xhat"][:, t, :], m["x"][:, b, t, :], m["mv"][:, t, 0:1],
                                 m["rstd"][:, t:t + 1], ALU.subtract, ALU.mult)
    last.then_inc(s["xhat"], 1)


def attention(nc, sem, m, a, tag, causal):
    w = a[tag]
    rotary = not causal
    names = ("loads", "w_raw", "w_hi", "w_lo", "w_rest", "focus", "ones", "stats", "mv", "var", "rstd", "xhat", "biased", "xT_ps", "xT", "q_ps", "q_main", "qr_ps",
             "q_turn", "q", "k_ps", "k_main", "kr_ps", "k_turn", "k", "v_ps", "v", "v_aug", "qh", "qr", "qm", "parts", "stored_q", "stored_k",
             "half0", "half1", "max_ps", "max", "nmh", "nm", "nm_ps0", "nm_ps1", "nm_row0", "nm_row1",
             "nm_out", "aug0", "aug1", "score", "prob", "pv", "o_raw", "o_out", "den", "rden", "rden_out",
             "o_in", "r_in", "oT", "proj", "resid")
    s = {n: sem(f"{tag}_{n}") for n in names}
    s["waited"] = m["waited"]
    own = ExitStack()

    def sb(name, shape, dt=F32):
        return own.enter_context(nc.sbuf_tensor(f"{tag}_{name}", shape, dt))

    m["xT"] = sb("xT", [P, S])
    m["weights"] = sb("weights", [P, 6, P])
    m["bias_col"] = sb("bias_col", [P, 4])
    m["bias_row"] = sb("bias_row", [P, 2, D])
    m["rope"] = sb("rope", [P, 4, S])
    m["stack_q"] = [sb(f"stack_q{c}", [P, PAIRS, S], BF16) for c in range(2)]
    m["v_aug"] = [sb(f"v_aug{c}", [P, T, H, HD + 1]) for c in range(2)]
    m["v"] = sb("v", [P, T, D])
    m["qf"] = sb("qf", [P, 2, S])
    m["turned"] = sb("turned", [P, 2, S])
    m["rest"] = sb("rest", [P, S])
    m["parts"] = sb("parts", [P, 2, 3, S], BF16)
    m["prob"] = [sb(f"prob{c}", [P, 4, S]) for c in range(2)]
    m["negmax"] = sb("negmax", [P, T, 2, PAIRS])
    m["nm_parts"] = sb("nm_parts", [P, T, 2, 2, 2, HALF], BF16)
    m["nm_rows"] = sb("nm_rows", [2 * 2 * HALF, 2, S], BF16)
    m["o_raw"] = sb("o_raw", [P, GROUPS, S])
    m["den"] = sb("den", [P, H * S // P])
    m["rden"] = sb("rden", [P, H * S // P])
    m["o_num"] = sb("o_num", [P, S])
    m["o_rden"] = sb("o_rden", [P, S])
    m["oT"] = sb("oT", [P, S])
    W_Q, W_K, W_V, W_QR, W_KR, W_O = range(6)

    def width(j):
        return P * j if causal else 0

    def pipeline(eng, step):
        for n in range(4):
            step(n, n % 2)
        with eng.Fori(2, B // 2) as i:
            step(2 * i, 0)
            step(2 * i + 1, 1)
        for n in range(B, B + 3):
            step(n, n % 2)

    def on(n, lag):
        return not isinstance(n, int) or 0 <= n - lag < B

    misc = [("nm_row1", 2), ("xT", 0)]
    misc += [("q_main", 0), ("q_turn", 0), ("k_main", 0), ("k_turn", 0)] if rotary else [("q", 0), ("k", 0)]
    misc += [("v", 0), ("nm_row0", 1), ("resid", 3)]
    user = {name: i for i, (name, _) in enumerate(misc)}

    def misc_free(pe, n, name):
        index, back = user[name], 0
        while True:
            index -= 1
            if index < 0:
                index, back = index + len(misc), back + 1
                if isinstance(n, int) and n - back < 0:
                    return
            before, lag = misc[index]
            if on(n - back if isinstance(n, int) else n, lag):
                pe.wait_ge(s[before], n - back - lag + 1)
                return

    def raw(i):
        place, name, cols = W_PIECES[i]
        k = cols // (D if name == "out" else F)
        if place == "o_raw":
            at = cols * (i - 2)
            return m["o_raw"][:].rearrange("p g t -> p (g t)")[:, at:at + cols].rearrange("p (k f) -> p k f", k=k)
        return m["prob"][i][:]

    with own, nc.Block() as block:

        @block.sync
        def _(sp):
            sp.dma_start(m["weights"][:, 0:6, :], w["w"].rearrange("n k m -> k n m")).then_inc(s["loads"], 16)
            sp.dma_start(m["bias_col"][:], w["bias_col"]).then_inc(s["loads"], 16)
            for i, name in enumerate(("bias_v", "bias_o")):
                sp.dma_start(m["bias_row"][:, i, :], w[name].partition_broadcast(P)).then_inc(s["loads"], 16)
            if rotary:
                sp.dma_start(m["rope"][:], w["rope"].rearrange("n p t -> p n t")).then_inc(s["loads"], 16)

            else:
                sp.dma_start(m["focus"][:], a["focus"]).then_inc(s["focus"], 16)

            def aug(n, h, b, c):
                wait_apart(sp, s, s[f"nm_row{h}"], b + 1)
                sp.dma_start(m["d_nm"][h].rearrange("o c p t -> (o c p) t"), m["nm_rows"][:, h, :])\
                    .then_inc(s["nm_out"], 16)
                wait_apart(sp, s, s["nm_out"], count(32, b, 16 * (h + 1)))
                for o in range(2):
                    at = AUG_AT + AUG * o
                    sp.dma_start(m["stack_q"][c][at:at + AUG, HALF * h:HALF * (h + 1), :],
                                 m["d_nm"][h, o]).then_inc(s[f"aug{h}"], 16)

            def step(n, c):
                if on(n, 2):
                    aug(n, 1, n - 2, c)
                if on(n, 3):
                    b = n - 3
                    wait_apart(sp, s, s["o_raw"], count(GROUPS, b, GROUPS))
                    for g in range(4):
                        sp.dma_start(m["d_num"][:, g], m["o_raw"][32 * g:32 * g + HD]).then_inc(s["o_out"], 16)
                        sp.dma_start(m["d_den"][g:g + 1], m["o_raw"][32 * g + HD:32 * g + HD + 1])\
                            .then_inc(s["o_out"], 16)
                    wait_apart(sp, s, s["o_out"], count(128, b, 128))
                    wait_apart(sp, s, s["rden"], b)
                    sp.dma_start(m["den"][:], m["d_den"].rearrange("g h (c t) -> (g h c) t", c=P // H))\
                        .then_inc(s["den"], 16)
                    wait_apart(sp, s, s["oT"], b)
                    sp.dma_start(m["o_num"][:], m["d_num"].rearrange("d g h t -> (d g h) t")).then_inc(s["o_in"], 16)
                    wait_apart(sp, s, s["rden"], b + 1)
                    sp.dma_start(m["d_rden"].rearrange("g h (c t) -> (g h c) t", c=P // H), m["rden"][:])\
                        .then_inc(s["rden_out"], 16)
                    wait_apart(sp, s, s["rden_out"], count(16, b, 16))
                    for d in range(HD):
                        sp.dma_start(m["o_rden"][H * d:H * (d + 1), :], m["d_rden"].rearrange("g h t -> (g h) t"))\
                            .then_inc(s["r_in"], 16)
                if on(n, 0):
                    b = n
                    for i, name in enumerate(("stored_q", "stored_k")):
                        wait_apart(sp, s, s["parts"], count(2, b, i + 1))
                        wait_apart(sp, s, s["half0"], count(64, b))
                        wait_apart(sp, s, s["half1"], count(64, b))
                        for o in range(2):
                            parts = m["parts"][64 * o:64 * (o + 1), i]
                            rows = m["d_stack"][i, o].rearrange("t d p n -> (d p) t n")
                            if i == 0:
                                for part, lo, hi in ((0, 0, 3), (1, 3, 5), (2, 5, 6)):
                                    sp.dma_start(rows[:, lo:hi],
                                                 parts[:, part:part + 1].broadcast_to([64, hi - lo, S]))\
                                        .then_inc(s[name], 16)
                            else:
                                for lo, hi in ((0, 3), (3, 5), (5, 6)):
                                    sp.dma_start(rows[:, lo:hi], parts[:, 0:hi - lo]).then_inc(s[name], 16)
                    wait_apart(sp, s, s["stored_q"], count(96, b, 96))
                    wait_apart(sp, s, s["stored_k"], count(96, b, 96))
                for h in range(2):
                    if on(n, 0):
                        b = n
                        wait_apart(sp, s, s["score"], count(4 * UNITS, b - 2, 2 * UNITS * (h + 1)))
                        pairs = slice(HALF * h, HALF * (h + 1))
                        for o in range(2):
                            q, k = (m["d_stack"][i, o].rearrange("t d p n -> (t d) p n") for i in range(2))
                            rows = slice(KROWS * o, KROWS * (o + 1))
                            sp.dma_start(m["stack_q"][c][rows, pairs, :], q[:, pairs, :])\
                                .then_inc(s[f"half{h}"], 16)
                            sp.dma_start(m["stack_k"][c][rows, o, pairs, :], k[:, pairs, :])\
                                .then_inc(s[f"half{h}"], 16)
                    if h == 0 and on(n, 1):
                        aug(n, 0, n - 1, 1 - c)

            if causal:
                for i, (place, name, cols) in enumerate(W_PIECES):
                    sp.dma_start(raw(i), a["w_" + name].rearrange("(k p) f -> p k f", p=P))\
                        .then_inc(s["w_raw"], 16)
            pipeline(sp, step)

        @block.gpsimd
        def _(pool):
            for c in range(2):
                last = pool.memset(m["v_aug"][c][:], 1.0)
            last.then_inc(s["ones"], 1)
            pool.wait_ge(s["loads"], 80 if rotary else 64)

            def step(n, c):
                if on(n, 2):
                    negated_max_parts(n - 2, 1)
                if on(n, 0):
                    b = n
                    norm_rstd(pool, m, s, b)
                    pool.wait_ge(s["xhat"], b + 1)
                    bias = m["bias_row"][:, 1:2, :].broadcast_to([P, T, D])
                    pool.tensor_tensor(m["x"][:, b], m["x"][:, b], bias, ALU.add).then_inc(s["biased"], 1)
                    for i, name in enumerate(("q", "k")):
                        if rotary:
                            pool.wait_ge(s[f"{name}_turn"], b + 1)
                            pool.wait_ge(s[f"{name}_main"], b + 1)
                            pool.tensor_tensor(m["qf"][:, i], m["qf"][:, i], m["turned"][:, i], ALU.add)\
                                .then_inc(s[name], 1)
                        pool.wait_ge(s[name], b + 1)
                        wait_apart(pool, s, s["stored_q" if i == 0 else "stored_k"], count(96, b))
                        full, part = m["qf"][:, i], m["parts"][:, i]
                        pool.tensor_copy(part[:, 0], full).then_inc(s["qh"], 1)
                        pool.wait_ge(s["qh"], count(2, b, i + 1))
                        pool.tensor_tensor(m["rest"][:], full, part[:, 0], ALU.subtract).then_inc(s["qr"], 1)
                        wait_apart(pool, s, s["qr"], count(2, b, i + 1))
                        pool.tensor_copy(part[:, 1], m["rest"][:]).then_inc(s["qm"], 1)
                        pool.wait_ge(s["qm"], count(2, b, i + 1))
                        pool.tensor_tensor(part[:, 2], m["rest"][:], part[:, 1], ALU.subtract).then_inc(s["parts"], 1)
                if on(n, 1):
                    negated_max_parts(n - 1, 0)
                if on(n, 3):
                    b = n - 3
                    pool.wait_ge(s["o_in"], count(16, b, 16))
                    pool.wait_ge(s["r_in"], count(16 * HD, b, 16 * HD))
                    wait(pool, s["proj"], b)
                    pool.tensor_tensor(m["oT"][:], m["o_num"][:], m["o_rden"][:], ALU.mult).then_inc(s["oT"], 1)
                if on(n, 0):
                    b = n
                    pool.wait_ge(s["v"], b + 1)
                    wait_apart(pool, s, s["pv"], count(UNITS, b - 1))
                    to, v = m["v_aug"][c], m["v"][:].rearrange("p t (h d) -> p t h d", h=H)
                    lo = FOCUS_HEADS if causal else 0
                    if causal:
                        pool.tensor_tensor(to[:, :, 0:lo, 0:HD], v[:, :, 0:lo],
                                           to[:, :, 0:lo, HD:HD + 1].broadcast_to([P, T, lo, HD]), ALU.mult)
                    pool.tensor_copy(to[:, :, lo:H, 0:HD], v[:, :, lo:H]).then_inc(s["v_aug"], 1)

            def negated_max_parts(b, h):
                pool.wait_ge(s["max"], count(MAXES, b, MAXES // 2 * (h + 1)))
                wait_apart(pool, s, s[f"nm_ps{h}"], b)
                full = m["negmax"][:, :, :, HALF * h:HALF * (h + 1)]
                parts = m["nm_parts"][:, :, h]
                pool.tensor_copy(parts[:, :, :, 0], full).then_inc(s["nmh"], 1)
                pool.wait_ge(s["nmh"], count(2, b, h + 1))
                pool.tensor_tensor(parts[:, :, :, 1], full, parts[:, :, :, 0], ALU.subtract).then_inc(s["nm"], 1)

            if causal:
                pool.wait_ge(s["focus"], 16)
                pool.wait_ge(s["ones"], 1)
                for c in range(2):
                    last = pool.tensor_copy(m["v_aug"][c][:, :, 0:FOCUS_HEADS, :],
                                            m["focus"][:].rearrange("p t (h o) -> p t h o", o=1)
                                            .broadcast_to([P, T, FOCUS_HEADS, HD + 1]))
                last.then_inc(s["ones"], 1)
                pool.wait_ge(s["ones"], 2)
            pipeline(pool, step)

        @block.vector
        def _(dve):
            dve.wait_ge(s["loads"], 80 if rotary else 64)

            def split_weights():
                dve.wait_ge(s["w_raw"], 16 * len(W_PIECES))
                for i, (_, name, cols) in enumerate(W_PIECES):
                    at = slice(W_AT[name], W_AT[name] + cols)
                    full = raw(i).rearrange("p k f -> p (k f)")
                    dve.tensor_copy(m["w_hi"][:, at], full).then_inc(s["w_hi"], 1)
                    dve.wait_ge(s["w_hi"], i + 1)
                    dve.tensor_tensor(m["w_lo"][:, at], full, m["w_hi"][:, at].bitcast(F32), ALU.subtract)\
                        .then_inc(s["w_lo"], 1)
                    dve.wait_ge(s["w_lo"], i + 1)
                    dve.tensor_reduce(m["w_rest"][:, i:i + 1], m["w_lo"][:, at].bitcast(F32), AX.X, ALU.max,
                                      apply_absolute_value=True).then_inc(s["w_rest"], 1)

            def project(b, name, i):
                if not rotary:
                    dve.wait_ge(s[f"{name}_ps"], b + 1)
                    wait(dve, s["parts"], count(2, b, i - 1))
                    dve.tensor_scalar(m["qf"][:, i], m["ps_misc"][:], m["bias_col"][:, i:i + 1],
                                      1.0 if i else SCALE, ALU.add, ALU.mult).then_inc(s[name], 1)
                    return
                dve.wait_ge(s[f"{name}_ps"], b + 1)
                wait(dve, s["parts"], count(2, b, i - 1))
                dve.scalar_tensor_tensor(out=m["qf"][:, i], in0=m["ps_misc"][:], scalar=m["bias_col"][:, i:i + 1],
                                         in1=m["rope"][:, 2 * i], op0=ALU.add, op1=ALU.mult)\
                    .then_inc(s[f"{name}_main"], 1)

            def turn(b, name, i):
                dve.wait_ge(s[f"{name}r_ps"], b + 1)
                wait(dve, s[name], b)
                dve.scalar_tensor_tensor(out=m["turned"][:, i], in0=m["ps_misc"][:],
                                         scalar=m["bias_col"][:, 2 + i:3 + i], in1=m["rope"][:, 2 * i + 1],
                                         op0=ALU.add, op1=ALU.mult).then_inc(s[f"{name}_turn"], 1)

            def max_of(b, k):
                p, t = k // T, k % T
                if k % (MAXES // 2) == 0:
                    wait(dve, s["nm"], count(2, b - 1, 1 + k // (MAXES // 2)))
                dve.wait_ge(s["max_ps"], count(MAXES, b, k + 1))
                keys = P * (t + 1) if causal else S
                dve.tensor_reduce(m["negmax"][:, t, :, p], m["ps_max"][:, 2 * (k % 2):2 * (k % 2) + 2, 0:keys],
                                  AX.X, ALU.max, negate=True).then_inc(s["max"], 1)

            def step(n, c):
                for u in range(UNITS):
                    if on(n, 0):
                        if u == 0:
                            norm_stats(dve, m, s, n)
                        if u == 2:
                            norm_apply(dve, m, s, n)
                        if u == SLOT["q"] + 1:
                            project(n, "q", 0)
                        if u == SLOT["k"] + 1:
                            project(n, "k", 1)
                        if rotary and u == SLOT["qr"] + 1:
                            turn(n, "q", 0)
                        if rotary and u == SLOT["kr"] + 1:
                            turn(n, "k", 1)
                        if u == SLOT["v"] + 1:
                            dve.wait_ge(s["v_ps"], n + 1)
                            wait(dve, s["v_aug"], n)
                            dve.tensor_tensor(m["v"][:], m["ps_misc"][:].rearrange("p (t d) -> p t d", t=T),
                                              m["bias_row"][:, 0:1, :].broadcast_to([P, T, D]), ALU.add)\
                                .then_inc(s["v"], 1)
                    if on(n, 3):
                        b = n - 3
                        if u == 5:
                            dve.wait_ge(s["den"], count(16, b, 16))
                            wait(dve, s["rden_out"], count(16, b))
                            dve.reciprocal(m["rden"][:], m["den"][:]).then_inc(s["rden"], 1)
                        if u == SLOT["proj"] + 1:
                            dve.wait_ge(s["proj"], b + 1)
                            dve.wait_ge(s["biased"], b + 1)
                            dve.tensor_tensor(m["x"][:, b], m["ps_misc"][:].rearrange("p (t d) -> p t d", t=T),
                                              m["x"][:, b], ALU.add).then_inc(s["resid"], 1)
                    if on(n, 1):
                        max_of(n - 1, 2 * u)
                        max_of(n - 1, 2 * u + 1)
                if causal and isinstance(n, int) and n == 0:
                    split_weights()

            pipeline(dve, step)

        @block.scalar
        def _(act):
            def nm_row(b, h):
                act.wait_ge(s[f"nm_ps{h}"], b + 1)
                wait(act, s["nm_out"], count(32, b - 1, 16 * (h + 1)))
                act.activation(m["nm_rows"][:, h, :], m["ps_misc"][0:16, 0:S // 2].bitcast(BF16), ACT.Copy)\
                    .then_inc(s[f"nm_row{h}"], 1)

            def group_out(b, G):
                act.wait_ge(s["pv"], count(UNITS, b, T * (G + 1)))
                wait(act, s["o_out"], count(128, b))
                act.activation(m["o_raw"][:, G], m["ps_out"][:], ACT.Copy).then_inc(s["o_raw"], 1)

            def step(n, c):
                if causal and isinstance(n, int) and n == 2:
                    act.wait_ge(s["w_rest"], len(W_PIECES))
                for u in range(UNITS):
                    if u == SLOT["nm1"] + 1 and on(n, 2):
                        nm_row(n - 2, 1)
                    if u == SLOT["nm0"] + 1 and on(n, 1):
                        nm_row(n - 1, 0)
                    if u == SLOT["xT"] + 1 and on(n, 0):
                        act.wait_ge(s["xT_ps"], n + 1)
                        wait(act, s["v_ps"], n)
                        act.activation(m["xT"][:], m["ps_misc"][:], ACT.Copy).then_inc(s["xT"], 1)
                    for g in range(4):
                        if g == 0 and u == 1 and on(n, 3):
                            group_out(n - 3, GROUPS - 1)
                        if not on(n, 2):
                            continue
                        b = n - 2
                        if g == 0 and u % T == 1 and u > T:
                            group_out(b, u // T - 1)
                        if g == 0:
                            wait(act, s["pv"], count(UNITS, b, u - 1))
                        act.wait_ge(s["score"], count(4 * UNITS, b, 4 * u + g + 1))
                        lo = width(u % T)
                        act.activation(m["prob"][u % 2][:, g, lo:S], m["ps_score"][:, g % 2, 0:S - lo], ACT.Exp)\
                            .then_inc(s["prob"], 1)

            pipeline(act, step)

        @block.tensor
        def _(pe):
            pe.wait_ge(s["loads"], 80 if rotary else 64)

            def score(b, c, u, g):
                G, j = u // T, u % T
                p, o = 2 * G + g // 2, g % 2
                if g == 0 and u % (UNITS // 2) == 0:
                    h = u // (UNITS // 2)
                    pe.wait_ge(s[f"half{h}"], count(64, b, 64))
                    pe.wait_ge(s[f"aug{h}"], count(32, b, 32))
                wait(pe, s["prob"], count(4 * UNITS, b, 4 * u + g - 1))
                lo, rows = width(j), slice(0, AUG_AT + 2 * AUG)
                last = pe.matmul(m["ps_score"][:, g % 2, 0:S - lo], m["stack_k"][c][rows, o, p, P * j:P * (j + 1)],
                                 m["stack_q"][c][rows, p, lo:S], start=True, stop=True)
                if causal:
                    last = pe.matmul(m["ps_score"][:, g % 2, 0:P], m["mask_k"][:], m["ident_b"][:],
                                     start=False, stop=True, skip_group_check=True)
                last.then_inc(s["score"], 1)

            def maxes(b, c, k, o):
                p, t = k // T, k % T
                if k % (MAXES // 2) == 0 and o == 0:
                    pe.wait_ge(s[f"half{k // (MAXES // 2)}"], count(64, b, 64))
                if o == 0:
                    wait(pe, s["max"], count(MAXES, b, k - 1))
                keys = P * (t + 1) if causal else S
                to = m["ps_max"][:, 2 * (k % 2) + o]
                last = pe.matmul(to[:, 0:keys], m["stack_q"][c][0:AUG_AT, p, P * t:P * (t + 1)],
                                 m["stack_k"][c][0:AUG_AT, o, p, 0:keys], start=True, stop=True)
                if causal:
                    last = pe.matmul(to[:, keys - P:keys], m["mask_q"][:], m["ident_b"][:],
                                     start=False, stop=True, skip_group_check=True)
                if o == 1:
                    last.then_inc(s["max_ps"], 1)

            def weigh(b, c, u):
                G, j = u // T, u % T
                if u == 0:
                    pe.wait_ge(s["v_aug"], b + 1)
                if j == 0:
                    wait(pe, s["o_raw"], count(GROUPS, b, G))
                pe.wait_ge(s["prob"], count(4 * UNITS, b, 4 * u + 4))
                lo = width(j)
                for g in range(4):
                    last = pe.matmul(m["ps_out"][32 * g:32 * g + HD + 1, lo:S], m["v_aug"][c][:, j, 4 * G + g, :],
                                     m["prob"][u % 2][:, g, lo:S], start=(j == 0), stop=(j == T - 1),
                                     skip_group_check=True)
                last.then_inc(s["pv"], 1)

            def turn_maxima(n, b, h):
                pe.wait_ge(s["nm"], count(2, b, h + 1))
                misc_free(pe, n, f"nm_row{h}")
                for t in range(T):
                    last = pe.transpose(m["ps_misc"][0:16, P // 2 * t:P // 2 * (t + 1)].bitcast(BF16),
                                        m["nm_parts"][:, t, h].rearrange("p a b c -> p (a b c)"), m["ident_b"][:])
                last.then_inc(s[f"nm_ps{h}"], 1)

            def linear(n, name, which, done):
                misc_free(pe, n, name)
                pe.wait_ge(s["xT"], n + 1)
                pe.matmul(m["ps_misc"][:], m["weights"][:, which], m["xT"][:], start=True, stop=True)\
                    .then_inc(s[done], 1)

            def misc_work(n, u):
                if u == SLOT["nm1"] and on(n, 2):
                    turn_maxima(n, n - 2, 1)
                if u == SLOT["nm0"] and on(n, 1):
                    turn_maxima(n, n - 1, 0)
                if u == SLOT["proj"] and on(n, 3):
                    pe.wait_ge(s["oT"], n - 3 + 1)
                    misc_free(pe, n, "resid")
                    for t in range(T):
                        last = pe.matmul(m["ps_misc"][:, P * t:P * (t + 1)], m["oT"][:, P * t:P * (t + 1)],
                                         m["weights"][:, W_O], start=True, stop=True)
                    last.then_inc(s["proj"], 1)
                if not on(n, 0):
                    return
                if u == SLOT["xT"]:
                    pe.wait_ge(s["xhat"], n + 1)
                    misc_free(pe, n, "xT")
                    for t in range(T):
                        last = pe.transpose(m["ps_misc"][:, P * t:P * (t + 1)], m["xhat"][:, t, :], m["ident"][:])
                    last.then_inc(s["xT_ps"], 1)
                if u == SLOT["q"]:
                    linear(n, "q_main" if rotary else "q", W_Q, "q_ps")
                if u == SLOT["k"]:
                    linear(n, "k_main" if rotary else "k", W_K, "k_ps")
                if rotary and u == SLOT["qr"]:
                    linear(n, "q_turn", W_QR, "qr_ps")
                if rotary and u == SLOT["kr"]:
                    linear(n, "k_turn", W_KR, "kr_ps")
                if u == SLOT["v"]:
                    misc_free(pe, n, "v")
                    for t in range(T):
                        last = pe.matmul(m["ps_misc"][:, P * t:P * (t + 1)], m["xT"][:, P * t:P * (t + 1)],
                                         m["weights"][:, W_V], start=True, stop=True)
                    last.then_inc(s["v_ps"], 1)

            def step(n, c):
                for u in range(UNITS):
                    if on(n, 1):
                        maxes(n - 1, 1 - c, 2 * u, 0)
                    if on(n, 2):
                        score(n - 2, c, u, 0)
                    if on(n, 1):
                        maxes(n - 1, 1 - c, 2 * u, 1)
                    if on(n, 2):
                        score(n - 2, c, u, 1)
                    if u == 0 and on(n, 3):
                        weigh(n - 3, 1 - c, UNITS - 1)
                    if u > 0 and on(n, 2):
                        weigh(n - 2, c, u - 1)
                    if on(n, 2):
                        score(n - 2, c, u, 2)
                    if on(n, 1):
                        maxes(n - 1, 1 - c, 2 * u + 1, 0)
                    if on(n, 2):
                        score(n - 2, c, u, 3)
                    if on(n, 1):
                        maxes(n - 1, 1 - c, 2 * u + 1, 1)
                    misc_work(n, u)

            pipeline(pe, step)


SLOT = {"nm1": 1, "xT": 3, "q": 4, "qr": 5, "k": 6, "kr": 7, "v": 8, "nm0": 12, "proj": 14}


def ffn(nc, sem, m, a, tag, out):
    names = ("halved", "flag", "stats", "mv", "var", "rstd", "xhat", "xT_ps", "xT_hi", "xT", "a_ps", "b_ps",
             "tanh", "ut", "h1f", "h1_hi", "h1", "l2_ps", "h2f", "h2_hi", "h2", "l3_ps", "h3f", "h3_hi", "h3",
             "y_ps", "y", "resid", "stored")
    s = {n: sem(f"{tag}_{n}") for n in names}
    s["waited"] = m["waited"]

    with ExitStack() as own:
        def sb(name, shape, dt=F32):
            return own.enter_context(nc.sbuf_tensor(f"{tag}_{name}", shape, dt))

        xT = sb("xT", [P, 2, S], F32R)
        tanh, ut, h1f = (sb(name, [P, 2, S]) for name in ("tanh", "ut", "h1f"))
        hf = {2: sb("h2f", [P, 2, S]), 3: sb("h3f", [P, 2, S])}
        h = {k: sb(f"h{k}", [P, 2, FT, S], F32R) for k in (1, 2, 3)}
        y = sb("y", [P, T, D])
        s_half, s_gate = sb("s_half", [P, FT]), sb("s_gate", [P, FT])
        flags, flag_f, flag = sb("flags", [P, 1]), sb("flag_f", [1, 1]), sb("flag", [1, 1], I32)
        w_hi, w_lo = m["w_hi"], m["w_lo"]

        def pipeline(eng, step):
            for n in range(3):
                step(n)
            with eng.Fori(3, B - 1) as n:
                step(n)
            for n in range(B - 1, B + 2):
                step(n)

        def on(n, lag):
            return not isinstance(n, int) or 0 <= n - lag < B

        with nc.Block() as block:

            @block.sync
            def _(sp):
                def step(n):
                    if on(n, 2):
                        wait_apart(sp, s, s["resid"], n - 1)
                        sp.dma_start(out[n - 2].rearrange("(t p) d -> p t d", p=P), m["x"][:, n - 2])\
                            .then_inc(s["stored"], 16)

                if out is not None:
                    pipeline(sp, step)
                    sp.wait_ge(s["stored"], 16 * B)

            @block.gpsimd
            def _(pool):
                def low(b, k):
                    for f in range(FT):
                        pool.wait_ge(s[f"h{k}_hi"], count(FT, b, f + 1))
                        pool.tensor_tensor(h[k][:, 1, f], hf[k][:, f % 2], h[k][:, 0, f], ALU.subtract)\
                            .then_inc(s[f"h{k}"], 1)

                def step(n):
                    if on(n, 1):
                        low(n - 1, 2)
                    if on(n, -1):
                        norm_rstd(pool, m, s, n + 1)
                    if on(n, 1):
                        low(n - 1, 3)

                norm_rstd(pool, m, s, 0)
                pipeline(pool, step)

            @block.vector
            def _(dve):
                dve.wait_ge(m["ffn_loaded"], m["ffn_loads"])
                dve.tensor_scalar(s_half[:], m["s_col"][:, 0], 0.5, None, ALU.mult).then_inc(s["halved"], 1)
                dve.wait_ge(s["halved"], 1)
                dve.tensor_tensor(s_gate[:], s_half[:], m["s_col"][:, 1], ALU.mult)
                dve.tensor_reduce(flags[:], m["w_rest"][:], AX.X, ALU.max).then_inc(s["halved"], 1)
                dve.wait_ge(s["flag"], 1)
                dve.tensor_reduce(flag_f[:], m["ps_misc"][0:1, 0:P], AX.X, ALU.max).then_inc(s["halved"], 1)
                dve.wait_ge(s["halved"], 3)
                dve.tensor_scalar(flag[:], flag_f[:], 0.0, None, ALU.is_gt).then_inc(s["halved"], 1)
                norm_stats(dve, m, s, 0)
                norm_apply(dve, m, s, 0)

                def gated(n, f):
                    dve.wait_ge(s["tanh"], count(FT, n, f + 1))
                    dve.scalar_tensor_tensor(out=ut[:, f % 2], in0=tanh[:, f % 2], scalar=1.0,
                                             in1=m["ps_a"][:, f % 2], op0=ALU.add, op1=ALU.mult)\
                        .then_inc(s["ut"], 1)
                    dve.wait_ge(s["ut"], count(FT, n, f + 1))
                    dve.wait_ge(s["b_ps"], count(FT, n, f + 1))
                    dve.scalar_tensor_tensor(out=h1f[:, f % 2], in0=m["ps_b"][:, f % 2],
                                             scalar=s_gate[:, f:f + 1], in1=ut[:, f % 2],
                                             op0=ALU.mult, op1=ALU.mult).then_inc(s["h1f"], 1)
                    dve.wait_ge(s["h1f"], count(FT, n, f + 1))
                    if f == 0:
                        wait(dve, s["l2_ps"], count(FT, n))
                    dve.tensor_copy(h[1][:, 0, f], h1f[:, f % 2]).then_inc(s["h1_hi"], 1)
                    dve.wait_ge(s["h1_hi"], count(FT, n, f + 1))
                    dve.tensor_tensor(h[1][:, 1, f], h1f[:, f % 2], h[1][:, 0, f], ALU.subtract)\
                        .then_inc(s["h1"], 1)

                def step(n):
                    if on(n, 0):
                        dve.wait_ge(s["xT_hi"], n + 1)
                        dve.tensor_tensor(xT[:, 1], m["ps_misc"][:], xT[:, 0], ALU.subtract).then_inc(s["xT"], 1)
                    if on(n, 2):
                        b = n - 2
                        wait(dve, s["resid"], b)
                        dve.wait_ge(s["y_ps"], b + 1)
                        dve.tensor_tensor(y[:], m["ps_out"][:].rearrange("p (t d) -> p t d", t=T),
                                          m["s3_row"][:].rearrange("p (o d) -> p o d", o=1)
                                          .broadcast_to([P, T, D]), ALU.mult).then_inc(s["y"], 1)
                        dve.wait_ge(s["y"], b + 1)
                        dve.tensor_tensor(m["x"][:, b], y[:], m["x"][:, b], ALU.add).then_inc(s["resid"], 1)
                    if on(n, -1):
                        norm_stats(dve, m, s, n + 1)
                    if on(n, 0):
                        gated(n, 0)
                        gated(n, 1)
                    if on(n, -1):
                        norm_apply(dve, m, s, n + 1)
                    if on(n, 0):
                        gated(n, 2)
                        gated(n, 3)

                pipeline(dve, step)

            @block.scalar
            def _(act):
                act.wait_ge(s["halved"], 2)

                def gelu(b, k, reader):
                    for f in range(FT):
                        act.wait_ge(s[f"l{k}_ps"], count(FT, b, f + 1))
                        wait(act, s[f"h{k}"], count(FT, b, f - 1))
                        act.activation(hf[k][:, f % 2], m["ps_hid"][:, f % 2], ACT.Gelu,
                                       scale=m["s_col"][:, k, f:f + 1]).then_inc(s[f"h{k}f"], 1)
                        act.wait_ge(s[f"h{k}f"], count(FT, b, f + 1))
                        if f == 0:
                            wait(act, s[reader], b if reader == "y_ps" else count(FT, b))
                        act.activation(h[k][:, 0, f], hf[k][:, f % 2], ACT.Copy).then_inc(s[f"h{k}_hi"], 1)

                def gate(n, f):
                    act.wait_ge(s["a_ps"], count(FT, n, f + 1))
                    wait(act, s["ut"], count(FT, n, f - 1))
                    act.activation(tanh[:, f % 2], m["ps_a"][:, f % 2], ACT.Tanh, scale=s_half[:, f:f + 1])\
                        .then_inc(s["tanh"], 1)

                def step(n):
                    if on(n, 0):
                        act.wait_ge(s["xT_ps"], n + 1)
                        wait(act, s["b_ps"], count(FT, n))
                        act.activation(xT[:, 0], m["ps_misc"][:], ACT.Copy).then_inc(s["xT_hi"], 1)
                    if on(n, 1):
                        gelu(n - 1, 2, "l3_ps")
                    if on(n, 0):
                        gate(n, 0)
                        gate(n, 1)
                    if on(n, 1):
                        gelu(n - 1, 3, "y_ps")
                    if on(n, 0):
                        gate(n, 2)
                        gate(n, 3)

                pipeline(act, step)

            @block.tensor
            def _(pe):
                pe.wait_ge(m["ffn_loaded"], m["ffn_loads"])
                pe.wait_ge(s["halved"], 2)
                pe.transpose(m["ps_misc"][0:1, 0:P], flags[:], m["ident"][:]).then_inc(s["flag"], 1)
                pe.wait_ge(s["halved"], 4)
                has_low = pe.value_load(flag[:], min_val=0, max_val=1)

                def program_of(whole):
                    weights = (w_hi, w_lo) if whole else (w_hi,)

                    def product(to, cols, moving, first, last):
                        pairs = [(w, part) for w in weights for part in range(2)]
                        for i, (w, part) in enumerate(pairs):
                            mm = pe.matmul(to, w[:, cols], moving(part), start=first and i == 0,
                                           stop=last and i == len(pairs) - 1)
                        return mm

                    def layer(b, k, freed):
                        for f in range(FT):
                            freed(f)
                            for i in range(FT):
                                if f == 0:
                                    pe.wait_ge(s[f"h{k - 1}"], count(FT, b, i + 1))
                                at = W_AT[f"h{k - 1}"] + F * i + P * f
                                mm = product(m["ps_hid"][:, f % 2], slice(at, at + P),
                                             lambda part: h[k - 1][:, part, i], i == 0, i == FT - 1)
                            mm.then_inc(s[f"l{k}_ps"], 1)

                    def gates(n, f):
                        for name, done, reader in (("a", "a_ps", "ut"), ("b", "b_ps", "h1f")):
                            wait(pe, s[reader], count(FT, n, f - 1))
                            at = W_AT[name] + P * f
                            product(m[f"ps_{name}"][:, f % 2], slice(at, at + P), lambda part: xT[:, part],
                                    True, True).then_inc(s[done], 1)

                    def step(n):
                        b = n - 1
                        if on(n, 0):
                            pe.wait_ge(s["xhat"], n + 1)
                            wait(pe, s["xT"], n)
                            for t in range(T):
                                mm = pe.transpose(m["ps_misc"][:, P * t:P * (t + 1)], m["xhat"][:, t, :],
                                                  m["ident"][:])
                            mm.then_inc(s["xT_ps"], 1)
                        if on(n, 2):
                            wait(pe, s["y"], n - 2)
                            for i in range(FT):
                                pe.wait_ge(s["h3"], count(FT, n - 2, i + 1))
                            for t in range(T):
                                for i in range(FT):
                                    pairs = [(w, part) for w in weights for part in range(2)]
                                    for q, (w, part) in enumerate(pairs):
                                        mm = pe.matmul(m["ps_out"][:, P * t:P * (t + 1)],
                                                       h[3][:, part, i, P * t:P * (t + 1)],
                                                       w[:, W_AT["out"] + D * i:W_AT["out"] + D * (i + 1)],
                                                       start=(i == 0 and q == 0),
                                                       stop=(i == FT - 1 and q == len(pairs) - 1))
                            mm.then_inc(s["y_ps"], 1)
                        if on(n, 1):
                            layer(b, 2, lambda f: wait(pe, s["h3f"], count(FT, b, f - 2)) if f < 2
                                  else pe.wait_ge(s["h2f"], count(FT, b, f - 1)))
                        if on(n, 0):
                            pe.wait_ge(s["xT"], n + 1)
                            gates(n, 0)
                            gates(n, 1)
                        if on(n, 1):
                            layer(b, 3, lambda f: pe.wait_ge(s["h2f"], count(FT, b, f + 3)) if f < 2
                                  else pe.wait_ge(s["h3f"], count(FT, b, f - 1)))
                        if on(n, 0):
                            gates(n, 2)
                            gates(n, 3)

                    pipeline(pe, step)

                with pe.If(has_low):
                    program_of(True)
                with pe.Else():
                    program_of(False)


def rows_of_heads():
    return np.array([(2 * p + o) * HD + d for o in range(2) for d in range(HD) for p in range(PAIRS)])


def rows_of_output():
    return np.array([(4 * G + g) * HD + d for d in range(HD) for g in range(4) for G in range(GROUPS)])


def rope_tables():
    inv = np.float32(1.0) / np.float32(10000.0) ** (np.arange(0, HD, 2, dtype=np.float32) / np.float32(HD))
    theta = np.arange(S, dtype=np.float32)[:, None] * inv[None, :].astype(np.float32)
    d = rows_of_heads() % HD
    cos, sin = np.cos(theta).T[d // 2], np.sin(theta).T[d // 2]
    sin = np.where((d % 2 == 0)[:, None], -sin, sin)
    scale = np.float32(SCALE)
    return np.stack([cos * scale, sin * scale, cos, sin]).astype(np.float32)


def focus_weights():
    edges = [0, max(1, S // 3), max(max(1, S // 3) + 1, 2 * S // 3), S]
    w = np.ones((P, T, FOCUS_HEADS), np.float32)
    for r in range(FOCUS_HEADS):
        for tok in range(edges[r], edges[r + 1]):
            w[tok % P, tok // P, r] = FOCUS
    return w


def turned_feature(f):
    return f ^ 1


def layout(i):
    q, o = rows_of_heads(), rows_of_output()
    qr = turned_feature(q)
    r = {"x": i["L0_attn_a_hidden_states"], "focus": focus_weights(), "rope": rope_tables()}
    w, bias = i["L0_attn_a_c_attn_w"], i["L0_attn_a_c_attn_b"]
    wq, wk, wv = w[:, 0:D], w[:, D:2 * D], w[:, 2 * D:3 * D]
    bq, bk = bias[0:D], bias[D:2 * D]
    r["a_w"] = np.stack([wq[:, q], wk[:, q], wv, wq[:, qr], wk[:, qr], i["L0_attn_a_c_proj_w"][o]])
    r["a_bias_col"] = np.stack([bq[q], bk[q], bq[qr], bk[qr]], 1)
    r["a_bias_v"], r["a_bias_o"] = bias[2 * D:3 * D], i["L0_attn_a_c_proj_b"]
    wq, wk, wv, wo = (i[f"L0_attn_b_W{n}"].T for n in "qkvo")
    bq, bk = i["L0_attn_b_bq"], i["L0_attn_b_bk"]
    r["b_w"] = np.stack([wq[:, q], wk[:, q], wv, wq[:, qr], wk[:, qr], wo[o]])
    r["b_bias_col"] = np.stack([bq[q], bk[q], bq[qr], bk[qr]], 1)
    r["b_bias_v"], r["b_bias_o"] = i["L0_attn_b_bv"], i["L0_attn_b_bo"]
    r["w_a"], r["w_b"] = i["L0_ffn_w1_w"].T, i["L0_ffn_w2_w"].T
    r["w_h1"], r["w_h2"], r["w_out"] = i["L0_ffn_h1_w"].T, i["L0_ffn_h2_w"].T, i["L0_ffn_w3_w"].T
    r["s_col"] = np.stack([i[f"L0_ffn_{n}_s"].reshape(FT, P).T for n in ("w1", "w2", "h1", "h2")], 1)
    r["s3"] = i["L0_ffn_w3_s"]
    return {k: np.ascontiguousarray(v) for k, v in r.items()}


def kernel(**inputs):
    import concourse.bacc as bacc
    from concourse.bass_utils import run_bass_kernel_spmd

    arrays = {f"in_{k}": v for k, v in layout({k: np.asarray(v) for k, v in inputs.items()}).items()}
    nc = bacc.Bacc("TRN2", target_bir_lowering=False, num_devices=1)
    a = {k[3:]: nc.dram_tensor(k, v.shape, mybir.dt.from_np(v.dtype), kind="ExternalInput").ap()
         for k, v in arrays.items()}
    for tag in "ab":
        a[tag] = {n: a[f"{tag}_{n}"] for n in ("w", "bias_col", "bias_v", "bias_o")}
        a[tag]["rope"] = a["rope"]
    out = nc.dram_tensor("out", (B, S, D), F32, kind="ExternalOutput").ap()
    program(nc, a, out)
    r = run_bass_kernel_spmd(nc, [arrays], core_ids=[0])
    return r.results[0]["out"]
```
